# Optimizing a Trainium2 kernel written in Bass

```python
import numpy as np
import jax
import jax.numpy as jnp

def _softmax(x, axis=-1):
    return jax.nn.softmax(x, axis=axis)

def _gelu(x):
    return jax.nn.gelu(x, approximate=True)

def _silu(x):
    return jax.nn.silu(x)

def _sigmoid(x):
    return jax.nn.sigmoid(x)

def _layernorm(x, axis=-1, eps=1e-05):
    m = jnp.mean(x, axis=axis, keepdims=True)
    v = jnp.var(x, axis=axis, keepdims=True)
    return (x - m) / jnp.sqrt(v + eps)

def _scatter_add(tgt, idx, src, axis=0):
    return tgt.at[idx].add(src)

def _segment_sum(src, seg, n):
    return jax.ops.segment_sum(src, seg, n)
kernel_name = 'mk_xattn_seq_d2_seqx_r8_ad8e8a'

def setup_inputs(seed: int=0):
    np.random.seed(seed)
    _w = jnp.asarray

    def _rec_inputs():
        import jax
        import jax.numpy as jnp
        _rk = jax.random.key(seed)
        x = 7.22e-05 + 1 * jax.random.normal(jax.random.fold_in(_rk, 1), (16, 128, 128), jnp.float32)
        _lenS = 128 - jax.random.randint(jax.random.fold_in(_rk, 7), (16,), 0, max(1, 128 // 4) + 1, jnp.int32)
        _lenS2 = 128 - jax.random.randint(jax.random.fold_in(_rk, 8), (16,), 0, max(1, 128 // 4) + 1, jnp.int32)
        _ctx_1024P = jax.random.normal(jax.random.fold_in(_rk, 11), (16, 16, 128), jnp.float32)
        _ctx_1024c = jax.random.dirichlet(jax.random.fold_in(_rk, 511), 0.3 * jnp.ones((16,), jnp.float32), (16, 128))
        _ctx_1024t = jnp.einsum('bsk,bkd->bsd', _ctx_1024c, _ctx_1024P)
        _ctx_1024t = _ctx_1024t * jax.lax.rsqrt(jnp.mean(jnp.square(_ctx_1024t)) + 1e-12) * 0.953939
        ctx_1024 = 4.13588e-05 + 0.999923 * (_ctx_1024t + 0.3 * jax.random.normal(jax.random.fold_in(_rk, 611), (16, 128, 128), jnp.float32))
        _validS = jnp.arange(128)[None, :] < _lenS[:, None]
        _validS2 = jnp.arange(128)[None, :] < _lenS2[:, None]
        _causal = jnp.tril(jnp.ones((128, 128), dtype=bool))
        mask_Bx1x1xS2_if1 = jnp.where(jnp.ones((16, 1, 1, 128), dtype=bool), 1, 0).astype(jnp.int32)
        mask_Bx1xSxS2_if1 = jnp.where(jnp.ones((16, 1, 128, 128), dtype=bool), 1, 0).astype(jnp.int32)
        return (x, ctx_1024, mask_Bx1x1xS2_if1, mask_Bx1xSxS2_if1)
    x, ctx_1024, mask_Bx1x1xS2_if1, mask_Bx1xSxS2_if1 = _rec_inputs()

    def _L0_xattn_setup():
        import jax, jax.numpy as jnp
        import numpy as np
        D_MODEL = 128
        NUM_HEADS = 16
        D_FF = 512
        D_K = D_MODEL // NUM_HEADS
        LN_EPS = 1e-05

        def _linear(x, w, b):
            return jnp.einsum('bsd,od->bso', x, w) + b

        def _layernorm(x, g, b):
            mu = jnp.mean(x, axis=-1, keepdims=True)
            var = jnp.mean(jnp.square(x - mu), axis=-1, keepdims=True)
            return (x - mu) * jax.lax.rsqrt(var + LN_EPS) * g + b

        def _mha(q_in, kv_in, mask, wq, bq, wk, bk, wv, bv, wo, bo):
            B, Sq, _ = q_in.shape
            Sk = kv_in.shape[1]
            q = _linear(q_in, wq, bq).reshape(B, Sq, NUM_HEADS, D_K).transpose(0, 2, 1, 3)
            k = _linear(kv_in, wk, bk).reshape(B, Sk, NUM_HEADS, D_K).transpose(0, 2, 1, 3)
            v = _linear(kv_in, wv, bv).reshape(B, Sk, NUM_HEADS, D_K).transpose(0, 2, 1, 3)
            scores = jnp.einsum('bhqd,bhkd->bhqk', q, k) / jnp.sqrt(jnp.asarray(D_K, q.dtype))
            scores = jnp.where(mask == 0, jnp.asarray(-1000000000.0, scores.dtype), scores)
            attn = jax.nn.softmax(scores, axis=-1)
            out = jnp.einsum('bhqk,bhkd->bhqd', attn, v)
            out = out.transpose(0, 2, 1, 3).reshape(B, Sq, D_MODEL)
            return _linear(out, wo, bo)
        key = jax.random.key(seed)
        ks = jax.random.split(key, 24)
        B, S = (4, 256)
        s = 0.02
        d = {'tgt': jax.random.normal(ks[0], (B, S, D_MODEL), jnp.float32), 'enc_output': jax.random.normal(ks[1], (B, S, D_MODEL), jnp.float32), 'src_mask': jnp.ones((B, 1, 1, S), jnp.int32), 'tgt_mask': jnp.ones((B, 1, S, S), jnp.int32)}
        names = ['sa_wq', 'sa_wk', 'sa_wv', 'sa_wo', 'ca_wq', 'ca_wk', 'ca_wv', 'ca_wo']
        for i, n in enumerate(names):
            d[n] = jax.random.normal(ks[2 + i], (D_MODEL, D_MODEL), jnp.float32) * s
            d[n.replace('w', 'b')] = jnp.zeros((D_MODEL,), jnp.float32)
        d['ffn_w1'] = jax.random.normal(ks[10], (D_FF, D_MODEL), jnp.float32) * s
        d['ffn_b1'] = jnp.zeros((D_FF,), jnp.float32)
        d['ffn_w2'] = jax.random.normal(ks[11], (D_MODEL, D_FF), jnp.float32) * s
        d['ffn_b2'] = jnp.zeros((D_MODEL,), jnp.float32)
        for i in (1, 2, 3):
            d[f'ln{i}_g'] = jnp.ones((D_MODEL,), jnp.float32)
            d[f'ln{i}_b'] = jnp.zeros((D_MODEL,), jnp.float32)
        return d
    _L0_xattn_all = _L0_xattn_setup()
    _L0_xattn_in = {k: v for k, v in _L0_xattn_all.items() if k in ('sa_wq', 'sa_bq', 'sa_wk', 'sa_bk', 'sa_wv', 'sa_bv', 'sa_wo', 'sa_bo', 'ca_wq', 'ca_bq', 'ca_wk', 'ca_bk', 'ca_wv', 'ca_bv', 'ca_wo', 'ca_bo', 'ffn_w1', 'ffn_b1', 'ffn_w2', 'ffn_b2', 'ln1_g', 'ln1_b', 'ln2_g', 'ln2_b', 'ln3_g', 'ln3_b')}
    del _L0_xattn_all

    def _L1_xattn_setup():
        import jax, jax.numpy as jnp
        import numpy as np
        EMBED = 128
        HEADS = 16
        HEAD_DIM = EMBED // HEADS
        LN_EPS = 1e-05

        def _split_heads(x):
            B, L, _ = x.shape
            return x.reshape(B, L, HEADS, HEAD_DIM).transpose(0, 2, 1, 3)
        key = jax.random.key(seed)
        ks = jax.random.split(key, 12)
        B, LQ, LK = (2, 256, 256)
        s = 1.0 / np.sqrt(EMBED)
        inp = {'query_seq': jax.random.normal(ks[0], (B, LQ, EMBED), jnp.float32), 'key_value_seq': jax.random.normal(ks[1], (B, LK, EMBED), jnp.float32), 'prompt_size': 0, 'Wq': jax.random.normal(ks[2], (EMBED, EMBED), jnp.float32) * s, 'bq': jnp.zeros((EMBED,), jnp.float32), 'Wk': jax.random.normal(ks[3], (EMBED, EMBED), jnp.float32) * s, 'bk': jnp.zeros((EMBED,), jnp.float32), 'Wv': jax.random.normal(ks[4], (EMBED, EMBED), jnp.float32) * s, 'bv': jnp.zeros((EMBED,), jnp.float32), 'Wo': jax.random.normal(ks[5], (EMBED, EMBED), jnp.float32) * s, 'bo': jnp.zeros((EMBED,), jnp.float32), 'ln_gamma': jnp.ones((EMBED,), jnp.float32), 'ln_beta': jnp.zeros((EMBED,), jnp.float32)}
        return inp
    _L1_xattn_all = _L1_xattn_setup()
    _L1_xattn_in = {k: v for k, v in _L1_xattn_all.items() if k in ('Wq', 'bq', 'Wk', 'bk', 'Wv', 'bv', 'Wo', 'bo', 'ln_gamma', 'ln_beta')}
    del _L1_xattn_all
    return {'x': x, 'ctx_1024': ctx_1024, 'mask_Bx1x1xS2_if1': mask_Bx1x1xS2_if1, 'mask_Bx1xSxS2_if1': mask_Bx1xSxS2_if1, 'L0_xattn_sa_wq': _L0_xattn_in['sa_wq'], 'L0_xattn_sa_bq': _L0_xattn_in['sa_bq'], 'L0_xattn_sa_wk': _L0_xattn_in['sa_wk'], 'L0_xattn_sa_bk': _L0_xattn_in['sa_bk'], 'L0_xattn_sa_wv': _L0_xattn_in['sa_wv'], 'L0_xattn_sa_bv': _L0_xattn_in['sa_bv'], 'L0_xattn_sa_wo': _L0_xattn_in['sa_wo'], 'L0_xattn_sa_bo': _L0_xattn_in['sa_bo'], 'L0_xattn_ca_wq': _L0_xattn_in['ca_wq'], 'L0_xattn_ca_bq': _L0_xattn_in['ca_bq'], 'L0_xattn_ca_wk': _L0_xattn_in['ca_wk'], 'L0_xattn_ca_bk': _L0_xattn_in['ca_bk'], 'L0_xattn_ca_wv': _L0_xattn_in['ca_wv'], 'L0_xattn_ca_bv': _L0_xattn_in['ca_bv'], 'L0_xattn_ca_wo': _L0_xattn_in['ca_wo'], 'L0_xattn_ca_bo': _L0_xattn_in['ca_bo'], 'L0_xattn_ffn_w1': _L0_xattn_in['ffn_w1'], 'L0_xattn_ffn_b1': _L0_xattn_in['ffn_b1'], 'L0_xattn_ffn_w2': _L0_xattn_in['ffn_w2'], 'L0_xattn_ffn_b2': _L0_xattn_in['ffn_b2'], 'L0_xattn_ln1_g': _L0_xattn_in['ln1_g'], 'L0_xattn_ln1_b': _L0_xattn_in['ln1_b'], 'L0_xattn_ln2_g': _L0_xattn_in['ln2_g'], 'L0_xattn_ln2_b': _L0_xattn_in['ln2_b'], 'L0_xattn_ln3_g': _L0_xattn_in['ln3_g'], 'L0_xattn_ln3_b': _L0_xattn_in['ln3_b'], 'L1_xattn_Wq': _L1_xattn_in['Wq'], 'L1_xattn_bq': _L1_xattn_in['bq'], 'L1_xattn_Wk': _L1_xattn_in['Wk'], 'L1_xattn_bk': _L1_xattn_in['bk'], 'L1_xattn_Wv': _L1_xattn_in['Wv'], 'L1_xattn_bv': _L1_xattn_in['bv'], 'L1_xattn_Wo': _L1_xattn_in['Wo'], 'L1_xattn_bo': _L1_xattn_in['bo'], 'L1_xattn_ln_gamma': _L1_xattn_in['ln_gamma'], 'L1_xattn_ln_beta': _L1_xattn_in['ln_beta']}

def reference(x, ctx_1024, mask_Bx1x1xS2_if1, mask_Bx1xSxS2_if1, L0_xattn_sa_wq, L0_xattn_sa_bq, L0_xattn_sa_wk, L0_xattn_sa_bk, L0_xattn_sa_wv, L0_xattn_sa_bv, L0_xattn_sa_wo, L0_xattn_sa_bo, L0_xattn_ca_wq, L0_xattn_ca_bq, L0_xattn_ca_wk, L0_xattn_ca_bk, L0_xattn_ca_wv, L0_xattn_ca_bv, L0_xattn_ca_wo, L0_xattn_ca_bo, L0_xattn_ffn_w1, L0_xattn_ffn_b1, L0_xattn_ffn_w2, L0_xattn_ffn_b2, L0_xattn_ln1_g, L0_xattn_ln1_b, L0_xattn_ln2_g, L0_xattn_ln2_b, L0_xattn_ln3_g, L0_xattn_ln3_b, L1_xattn_Wq, L1_xattn_bq, L1_xattn_Wk, L1_xattn_bk, L1_xattn_Wv, L1_xattn_bv, L1_xattn_Wo, L1_xattn_bo, L1_xattn_ln_gamma, L1_xattn_ln_beta):
    import jax
    import jax.numpy as jnp

    def _L0_xattn_ref(tgt, enc_output, src_mask, tgt_mask, sa_wq, sa_bq, sa_wk, sa_bk, sa_wv, sa_bv, sa_wo, sa_bo, ca_wq, ca_bq, ca_wk, ca_bk, ca_wv, ca_bv, ca_wo, ca_bo, ffn_w1, ffn_b1, ffn_w2, ffn_b2, ln1_g, ln1_b, ln2_g, ln2_b, ln3_g, ln3_b):
        import jax, jax.numpy as jnp
        import numpy as np
        D_MODEL = 128
        NUM_HEADS = 16
        D_FF = 512
        D_K = D_MODEL // NUM_HEADS
        LN_EPS = 1e-05

        def _linear(x, w, b):
            return jnp.einsum('bsd,od->bso', x, w) + b

        def _layernorm(x, g, b):
            mu = jnp.mean(x, axis=-1, keepdims=True)
            var = jnp.mean(jnp.square(x - mu), axis=-1, keepdims=True)
            return (x - mu) * jax.lax.rsqrt(var + LN_EPS) * g + b

        def _mha(q_in, kv_in, mask, wq, bq, wk, bk, wv, bv, wo, bo):
            B, Sq, _ = q_in.shape
            Sk = kv_in.shape[1]
            q = _linear(q_in, wq, bq).reshape(B, Sq, NUM_HEADS, D_K).transpose(0, 2, 1, 3)
            k = _linear(kv_in, wk, bk).reshape(B, Sk, NUM_HEADS, D_K).transpose(0, 2, 1, 3)
            v = _linear(kv_in, wv, bv).reshape(B, Sk, NUM_HEADS, D_K).transpose(0, 2, 1, 3)
            scores = jnp.einsum('bhqd,bhkd->bhqk', q, k) / jnp.sqrt(jnp.asarray(D_K, q.dtype))
            scores = jnp.where(mask == 0, jnp.asarray(-1000000000.0, scores.dtype), scores)
            attn = jax.nn.softmax(scores, axis=-1)
            out = jnp.einsum('bhqk,bhkd->bhqd', attn, v)
            out = out.transpose(0, 2, 1, 3).reshape(B, Sq, D_MODEL)
            return _linear(out, wo, bo)
        t2 = _mha(tgt, tgt, tgt_mask, sa_wq, sa_bq, sa_wk, sa_bk, sa_wv, sa_bv, sa_wo, sa_bo)
        x = _layernorm(tgt + t2, ln1_g, ln1_b)
        t2 = _mha(x, enc_output, src_mask, ca_wq, ca_bq, ca_wk, ca_bk, ca_wv, ca_bv, ca_wo, ca_bo)
        x = _layernorm(x + t2, ln2_g, ln2_b)
        t2 = _linear(jax.nn.relu(_linear(x, ffn_w1, ffn_b1)), ffn_w2, ffn_b2)
        return _layernorm(x + t2, ln3_g, ln3_b)

    def _L1_xattn_ref(query_seq, key_value_seq, prompt_size, Wq, bq, Wk, bk, Wv, bv, Wo, bo, ln_gamma, ln_beta):
        import jax, jax.numpy as jnp
        import numpy as np
        EMBED = 128
        HEADS = 16
        HEAD_DIM = EMBED // HEADS
        LN_EPS = 1e-05

        def _split_heads(x):
            B, L, _ = x.shape
            return x.reshape(B, L, HEADS, HEAD_DIM).transpose(0, 2, 1, 3)
        q = _split_heads(query_seq @ Wq.T + bq)
        k = _split_heads(key_value_seq @ Wk.T + bk)
        v = _split_heads(key_value_seq @ Wv.T + bv)
        scores = jnp.einsum('bhqd,bhkd->bhqk', q, k) / np.sqrt(HEAD_DIM).astype(np.float32)
        attn = jax.nn.softmax(scores, axis=-1)
        ctx = jnp.einsum('bhqk,bhkd->bhqd', attn, v)
        B, H, LQ, Dh = ctx.shape
        ctx = ctx.transpose(0, 2, 1, 3).reshape(B, LQ, H * Dh)
        out = ctx @ Wo.T + bo
        x = out + query_seq
        mu = jnp.mean(x, axis=-1, keepdims=True)
        var = jnp.var(x, axis=-1, keepdims=True)
        return (x - mu) * jax.lax.rsqrt(var + LN_EPS) * ln_gamma + ln_beta
    x = _L0_xattn_ref(x, ctx_1024, mask_Bx1x1xS2_if1, mask_Bx1xSxS2_if1, L0_xattn_sa_wq, L0_xattn_sa_bq, L0_xattn_sa_wk, L0_xattn_sa_bk, L0_xattn_sa_wv, L0_xattn_sa_bv, L0_xattn_sa_wo, L0_xattn_sa_bo, L0_xattn_ca_wq, L0_xattn_ca_bq, L0_xattn_ca_wk, L0_xattn_ca_bk, L0_xattn_ca_wv, L0_xattn_ca_bv, L0_xattn_ca_wo, L0_xattn_ca_bo, L0_xattn_ffn_w1, L0_xattn_ffn_b1, L0_xattn_ffn_w2, L0_xattn_ffn_b2, L0_xattn_ln1_g, L0_xattn_ln1_b, L0_xattn_ln2_g, L0_xattn_ln2_b, L0_xattn_ln3_g, L0_xattn_ln3_b)
    x = _L1_xattn_ref(x, ctx_1024, 0, L1_xattn_Wq, L1_xattn_bq, L1_xattn_Wk, L1_xattn_bk, L1_xattn_Wv, L1_xattn_bv, L1_xattn_Wo, L1_xattn_bo, L1_xattn_ln_gamma, L1_xattn_ln_beta)
    return x

_drawn_inputs = setup_inputs


def setup_inputs(seed=0):
    import zlib

    import numpy as np

    out = dict(_drawn_inputs(seed))
    spreads = {'L0_xattn_sa_bq': (0.0, 0.8),
     'L0_xattn_sa_bk': (0.0, 2.0),
     'L0_xattn_sa_bv': (0.0, 0.408),
     'L0_xattn_sa_bo': (0.0, 0.1),
     'L0_xattn_ca_bq': (0.0, 2.0),
     'L0_xattn_ca_bk': (0.0, 2.0),
     'L0_xattn_ca_bv': (0.0, 0.366),
     'L0_xattn_ca_bo': (0.0, 0.1),
     'L0_xattn_ffn_b1': (0.0, 0.315),
     'L0_xattn_ffn_b2': (0.0, 0.1),
     'L0_xattn_ln1_g': (1.0, 0.2),
     'L0_xattn_ln1_b': (0.0, 0.1),
     'L0_xattn_ln2_g': (1.0, 0.2),
     'L0_xattn_ln2_b': (0.0, 0.1),
     'L0_xattn_ln3_g': (1.0, 0.2),
     'L0_xattn_ln3_b': (0.0, 0.1),
     'L1_xattn_bq': (0.0, 0.39),
     'L1_xattn_bk': (0.0, 2.0),
     'L1_xattn_bv': (0.0, 0.1),
     'L1_xattn_bo': (0.0, 0.1),
     'L1_xattn_ln_gamma': (1.0, 0.2),
     'L1_xattn_ln_beta': (0.0, 0.1)}
    factors = {'L0_xattn_sa_wq': 8.0,
     'L0_xattn_sa_wk': 8.0,
     'L0_xattn_sa_wv': 8.0,
     'L0_xattn_sa_wo': 2.789,
     'L0_xattn_ca_wq': 8.0,
     'L0_xattn_ca_wk': 8.0}
    for name, (base, spread) in spreads.items():
        noise = np.random.default_rng([zlib.crc32(name.encode()), seed]).standard_normal(out[name].shape)
        drawn = base * np.exp(spread * noise) if base else spread * noise
        out[name] = jnp.asarray(drawn.astype(out[name].dtype))
    for name, factor in factors.items():
        out[name] = (out[name] * factor).astype(out[name].dtype)
    return out
```

```python
import concourse.bass as bass
from concourse import mybir
from contextlib import ExitStack

F32 = mybir.dt.float32
BF16 = mybir.dt.bfloat16
I32 = mybir.dt.int32
U32 = mybir.dt.uint32
ALU = mybir.AluOpType
ACT = mybir.ActivationFunctionType
AX = mybir.AxisListType

B, S, D, H, DK, FF = 16, 128, 128, 16, 8, 512
PAIRS = H // 2
LAYERS = 3
GB = 4
GT = GB * S
NG = B // GB
UNITS, GROUPS = LAYERS * B, LAYERS * NG
CH = H // 4
NPROD = 6
Q_PART = [0, 0, 0, 1, 1, 2]
K_PART = [0, 1, 2, 0, 1, 0]
MASK_ROW = 16 * NPROD
MAX_ROW = MASK_ROW + 1
K_SCORES = MAX_ROW
SCALE = float(1.0 / DK ** 0.5)
NEG = -float(2 ** 30)
EPS = 1e-5
STACKS = 3
PROBS = 6

WQ, WK, WV, WO, W1, W2 = 0, 3 * D, 6 * D, 9 * D, 12 * D, 12 * D + FF
WCOLS = W2 + FF
VBQ, VBK, VBV, VB1, VG, VB = 0, 3, 6, 9, 13, 16
VCOLS = 19
R_BOSA, R_G, R_B, R_BO = 0, 1, 5, 9
ROWS = 12
BK_S, BK_ST, BK_PV, BK_X, BK_G, BK_Y = 0, 2, 4, 5, 6, 7


def schedule():
    tasks = []
    for g in range(GROUPS):
        s = 4 * g
        tasks += [(s - 8, 2, "K", g), (s - 8, 3, "V", g), (s - 7, 3, "Q", g)]
        if g < NG:
            tasks += [(s - 8, 0, "A", g)]
        else:
            tasks += [(s - 7, 2, "X", g)]
        if g >= 2 * NG:
            tasks += [(s - 9, 0, "FX", g), (s - 9, 1, "H0", g), (s - 9, 2, "H1", g), (s - 9, 3, "H2", g),
                      (s - 8, 0, "H3", g), (s - 8, 1, "F2", g)]
    return sorted(tasks)


def build(nc, x_tok, x_t, ctx_t, mask_k, mask_qk, weights, vectors, rows, k_rows, q_rows, ident_in, out):
    tasks = schedule()
    index = {(kind, g): n for n, (_, _, kind, g) in enumerate(tasks)}
    at = {(slot, step): (kind, g) for slot, step, kind, g in tasks}
    first_slot, last_slot = -8, UNITS + 3
    steps = [(s, i) for s in range(first_slot, last_slot + 1) for i in range(CH)]

    ctx = ExitStack()
    with ctx:
        def sb(name, shape, dt=F32):
            return ctx.enter_context(nc.sbuf_tensor(name, shape, dt))

        def sem(name):
            return ctx.enter_context(nc.semaphore(name))

        w = sb("w", [128, WCOLS])
        vec = sb("vec", [128, VCOLS])
        row = sb("row", [128, ROWS, D])
        ident = sb("ident", [128, 128])
        identb = sb("identb", [128, 128], BF16)
        xt = sb("xt", [128, B * S])
        ct = sb("ct", [128, B * S])
        res = sb("res", [128, B, D])
        norm = sb("norm", [128, B, D])
        rsum = sb("rsum", [128, 2, GB, D])
        stat = sb("stat", [128, GB, 6])
        mv = sb("mv", [128, GB, 2])
        fstat = sb("fstat", [128, GB, 6])
        fmv = sb("fmv", [128, GB, 2])
        rstd = sb("rstd", [128, 2, GB])
        vareps = sb("vareps", [128, 2, GB])
        mhalf = sb("mhalf", [128, GB])
        xg = sb("xg", [128, GT])
        hid = sb("hid", [128, 4, GT])
        qst = [sb(f"qst{n}", [128, PAIRS, GT], BF16) for n in range(STACKS)]
        kst = [sb(f"kst{n}", [128, PAIRS, 2, GT], BF16) for n in range(STACKS)]
        vst = [sb(f"vst{n}", [128, GB, H, 32]) for n in range(STACKS)]
        full = {m: sb(f"full{m}", [128, GT]) for m in "QK"}
        rest = {m: sb(f"rest{m}", [128, GT]) for m in "QK"}
        part = {m: sb(f"part{m}", [128, 3, GT], BF16) for m in "QK"}
        probs = sb("probs", [128, PROBS, 4, S])
        qscale = sb("qscale", [128, GT])
        cscale = sb("cscale", [128, B])
        anyk = sb("anyk", [128, B], BF16)
        anyf = sb("anyf", [128, B])
        mqk = sb("mqk", [128, B, S], BF16)
        mk = sb("mk", [128, B, S], BF16)
        zrow = sb("zrow", [1, GT], BF16)
        negm = sb("negm", [128, 2, H])
        nrest = sb("nrest", [128, 2, H])
        nparts = sb("nparts", [128, 3, H], BF16)
        mt = sb("mt", [48, 2, S], BF16)
        o9 = sb("o9", [128, CH, S])
        rec = sb("rec", [128, H])
        onorm = sb("onorm", [128, D])
        onT = sb("onT", [128, S])
        fin = sb("fin", [128, 2, GB, D])
        ps = ctx.enter_context(nc.psum_tensor("ps", [128, 8, 512], F32))
        mqk_in = norm[:, :, :].bitcast(I32)
        mk_in = hid[:, :, :].bitcast(I32).rearrange("p a (b k) -> p (a b) k", k=S)

        ld_w, ld_vec, ld_row, ld_id = sem("ld_w"), sem("ld_vec"), sem("ld_row"), sem("ld_id")
        ld_x, ld_c, ld_res, ld_mqk, ld_mk = sem("ld_x"), sem("ld_c"), sem("ld_res"), sem("ld_mqk"), sem("ld_mk")
        zeroed = [sem(f"zeroed{n}") for n in range(STACKS)]
        ld_rows = [sem(f"ld_rows{n}") for n in range(STACKS)]
        stacked = [sem(f"stacked{n}") for n in range(STACKS)]
        ident_ready, const_ready, masks_ready = sem("ident_ready"), sem("const_ready"), sem("masks_ready")
        mask_step, bias_rows = sem("mask_step"), sem("bias_rows")
        g_ready, g_evac = sem("g_ready"), sem("g_evac")
        s_ready, max_done = sem("s_ready"), sem("max_done")
        nparts_step, nparts_done, mt_ready, mt_evac = sem("nparts_step"), sem("nparts_done"), sem("mt_ready"), sem("mt_evac")
        max_loaded = [sem("max_loaded0"), sem("max_loaded1")]
        st_ready, exp_done, pv_done, o9_evac = sem("st_ready"), sem("exp_done"), sem("pv_done"), sem("o9_evac")
        ox_ready, rec_done, onorm_done, ot_ready, ot_evac = (
            sem("ox_ready"), sem("rec_done"), sem("onorm_done"), sem("ot_ready"), sem("ot_evac"))
        wo_ready, resid_done, stat_done, mv_done = sem("wo_ready"), sem("resid_done"), sem("stat_done"), sem("mv_done")
        fres_done, fstat_done, fmv_done = sem("fres_done"), sem("fstat_done"), sem("fmv_done")
        vareps_done, rstd_done, norm_done, gain_done, res_done = (
            sem("vareps_done"), sem("rstd_done"), sem("norm_done"), sem("gain_done"), sem("res_done"))
        p1 = {m: sem(f"part1_{m}") for m in "QK"}
        r1 = {m: sem(f"rest_{m}") for m in "QK"}
        p2 = {m: sem(f"part2_{m}") for m in "QK"}
        p3 = {m: sem(f"part3_{m}") for m in "QK"}
        fin_ready, stored = sem("fin_ready"), [sem("stored0"), sem("stored1")]

        def dmas_before(g):
            return sum(18 + (1 if mask_dma(o) else 0) for o in range(g % STACKS, g, STACKS))

        def mask_dma(g):
            return NG <= g < 2 * NG or 2 * NG <= g < 2 * NG + STACKS

        def all_stacked(g):
            return 16 * (dmas_before(g) + 18 + (1 if mask_dma(g) else 0))

        def norm_index(layer, g):
            return norm_order.index((layer, g))

        norm_order = []
        for s, i in steps:
            u = s - 3
            if i == 2 and 0 <= u < UNITS and u % 4 == 3:
                norm_order.append((u // B, (u // 4) % NG))
            if i == 3 and at.get((s, 1), ("", 0))[0] == "F2":
                norm_order.append(("F", at[(s, 1)][1] % NG))
        res_order = [(0, g) for g in range(NG)]
        for layer, g in norm_order:
            if layer != 2:
                res_order.append(({0: 1, 1: "F", "F": 2}[layer], g))
        source = {1: 0, 2: "F"}

        block = ctx.enter_context(nc.Block())

        @block.sync
        def _(sp):
            sp.dma_start(xt[:, :], x_t).then_inc(ld_x, 16)
            sp.dma_start(w[:, :], weights).then_inc(ld_w, 16)
            sp.dma_start(vec[:, :], vectors).then_inc(ld_vec, 16)
            sp.dma_start(ident[:, :], ident_in).then_inc(ld_id, 16)
            sp.dma_start(mqk_in, mask_qk.rearrange("b q k -> q b k")).then_inc(ld_mqk, 16)
            for n in range(STACKS):
                sp.wait_ge(zeroed[n], 2)
                sp.dma_start(kst[n][MASK_ROW:128, :, :, :], k_rows).then_inc(ld_rows[n], 16)
                sp.dma_start(qst[n][MASK_ROW:128, :, :], q_rows).then_inc(ld_rows[n], 16)
                if n == 0:
                    sp.dma_start(res[:, :, :], x_tok.rearrange("b t d -> t b d")).then_inc(ld_res, 16)
                    sp.dma_start(row[:, :, :], rows.partition_broadcast(128)).then_inc(ld_row, 16)
                if n == 1:
                    sp.dma_start(ct[:, :], ctx_t).then_inc(ld_c, 16)
                    sp.dma_start(mk_in, mask_k.partition_broadcast(128)).then_inc(ld_mk, 16)

            def stack_free(g):
                if g >= STACKS:
                    sp.wait_ge(st_ready, 4 * CH * (g - STACKS + 1))
                else:
                    sp.wait_ge(ld_rows[g], 32)

            def stack_k(g, c):
                for a in range(2):
                    sp.dma_start(kst[g % STACKS][16 * c + 8 * a:16 * c + 8 * a + 8, :, a, :],
                                 part["K"][64 * a:64 * a + 64, K_PART[c], :]).then_inc(stacked[g % STACKS], 16)

            def stack_q(g, c):
                sp.dma_start(qst[g % STACKS][16 * c:16 * c + 16, :, :],
                             part["Q"][:, Q_PART[c], :]).then_inc(stacked[g % STACKS], 16)

            for s, i in steps:
                if i == 2 and 0 <= s + 1 < UNITS:
                    u = s + 1
                    g, b = u // 4, u % 4
                    sp.wait_ge(mt_evac, u + 1)
                    sp.dma_start(qst[g % STACKS][MAX_ROW:MAX_ROW + 6, :, b * S:(b + 1) * S],
                                 mt[:, u % 2, :]).then_inc(max_loaded[u % 2], 16)
                if (s + 7) % 4 == 0 and i == 3 or (s + 6) % 4 == 0 and i < 3:
                    g, n = ((s + 7) // 4, 0) if i == 3 else ((s + 6) // 4, i + 1)
                    if 0 <= g < GROUPS and n < 3:
                        if n == 0:
                            stack_free(g)
                            sp.wait_ge(p3["K"], g + 1)
                            if mask_dma(g):
                                src = zrow[0:1, :]
                                if g < 2 * NG:
                                    sp.wait_ge(bias_rows, 1)
                                    src = mk[0:1, :, :].rearrange("p b k -> p (b k)")[:, (g % NG) * GT:(g % NG + 1) * GT]
                                sp.dma_start(kst[g % STACKS][MASK_ROW:MASK_ROW + 1, :, :, :].rearrange("o p a t -> o (p a) t"),
                                             src.unsqueeze(1).to_broadcast([1, 2 * PAIRS, GT])).then_inc(stacked[g % STACKS], 16)
                        stack_k(g, 2 * n)
                        stack_k(g, 2 * n + 1)
                if (s + 5) % 4 == 0 and i < 3:
                    g = (s + 5) // 4
                    if 0 <= g < GROUPS:
                        if i == 0:
                            sp.wait_ge(p3["Q"], g + 1)
                        stack_q(g, 2 * i)
                        stack_q(g, 2 * i + 1)
                if i == 3 and 0 <= s - 3 and s - 3 < UNITS and s - 3 >= 2 * B and (s - 3) % 4 == 3:
                    g = (s - 3 - 2 * B) // 4
                    sp.wait_ge(fin_ready, g + 1)
                    sp.dma_start(out[GB * g:GB * g + GB].rearrange("b t d -> t b d"),
                                 fin[:, g % 2, :, :]).then_inc(stored[g % 2], 16)
            sp.wait_ge(stored[0], 16 * (NG // 2))
            sp.wait_ge(stored[1], 16 * (NG // 2))

        @block.tensor
        def _(pe):
            mm = nc.tensor.matmul

            def scores(u, i):
                g, b, n = u // 4, u % 4, CH * u + i
                q, k, tok = qst[g % STACKS], kst[g % STACKS], slice(b * S, (b + 1) * S)
                if b == 0 and i == 0:
                    pe.wait_ge(stacked[g % STACKS], all_stacked(g))
                    if g < STACKS:
                        pe.wait_ge(ld_rows[g], 32)
                if n >= 2:
                    pe.wait_ge(max_done, n - 1)
                bank = ps[:, BK_S + n % 2, :]
                masked = u < B
                if masked:
                    if n == 0:
                        pe.wait_ge(masks_ready, 1)
                        pe.wait_ge(ident_ready, 1)
                    mm(bank.rearrange("p (h k) -> p h k", h=4), identb[:, :],
                       mqk[:, u, :].unsqueeze(1).to_broadcast([128, 4, S]), start=True, stop=False, skip_group_check=True)
                for j in range(2):
                    p = 2 * i + j
                    last = mm(bank[:, 256 * j:256 * j + 256].rearrange("p (a k) -> p a k", a=2), q[0:K_SCORES, p, tok],
                              k[0:K_SCORES, p, :, tok], start=not masked, stop=True, skip_group_check=True)
                last.then_inc(s_ready, 1)

            def shifted_scores(u, i):
                g, b, n = u // 4, u % 4, CH * u + i
                q, k, tok = qst[g % STACKS], kst[g % STACKS], slice(b * S, (b + 1) * S)
                if i == 0:
                    pe.wait_ge(max_loaded[u % 2], 16 * (u // 2 + 1))
                if n >= 2:
                    pe.wait_ge(exp_done, n - 1)
                bank = ps[:, BK_ST + n % 2, :]
                masked = u < B
                if masked:
                    mm(bank.rearrange("p (h q) -> p h q", h=4), mqk[:, u, :],
                       identb[:, :].unsqueeze(1).to_broadcast([128, 4, S]), start=True, stop=False, skip_group_check=True)
                for c in range(4):
                    p, a = 2 * i + c // 2, c % 2
                    last = mm(bank[:, c * S:(c + 1) * S], k[:, p, a, tok], q[:, p, tok],
                              start=not masked, stop=True, skip_group_check=True)
                last.then_inc(st_ready, 1)

            def values(n):
                u, i = n // CH, n % CH
                g, b = u // 4, u % 4
                pe.wait_ge(exp_done, n + 1)
                if i == 0:
                    if b == 0:
                        pe.wait_ge(g_evac, index["V", g] + 1)
                    if u > 0:
                        pe.wait_ge(o9_evac, u)
                    else:
                        pe.wait_ge(const_ready, 1)
                for c in range(4):
                    last = mm(ps[32 * c:32 * c + 32, BK_PV, i * S:(i + 1) * S], vst[g % STACKS][:, b, 4 * i + c, :],
                              probs[:, n % PROBS, c, :], start=True, stop=True, tile_position=(0, 32 * c))
                last.then_inc(pv_done, 1)

            def transposed_rows(source_rows, g, n):
                pe.wait_ge(norm_done, n + 1)
                for b in range(GB):
                    last = nc.tensor.transpose(ps[:, BK_G, b * S:(b + 1) * S], source_rows[:, GB * (g % NG) + b, :], ident[:, :])
                return last

            def group_task(kind, g):
                layer, gg = g // NG, g % NG
                n = index[kind, g]
                if n > 0:
                    pe.wait_ge(g_evac, n)
                bank = ps[:, BK_G, :]
                ctxs = xt if layer == 0 else ct
                tok = slice(gg * GT, (gg + 1) * GT)
                if kind in "KV" and g == NG:
                    pe.wait_ge(ld_c, 16)
                if kind == "A":
                    pe.wait_ge(mask_step, 2)
                    pe.wait_ge(ident_ready, 1)
                    for b in range(GB):
                        last = mm(bank[:, b * S:(b + 1) * S], anyk[:, GB * gg + b:GB * gg + b + 1].to_broadcast([128, 128]),
                                  identb[:, :], start=True, stop=True)
                elif kind == "K":
                    if g == 0:
                        pe.wait_ge(ld_w, 16)
                        pe.wait_ge(ld_x, 16)
                    last = mm(bank, w[:, WK + layer * D:WK + (layer + 1) * D], ctxs[:, tok], start=True, stop=True)
                elif kind == "V":
                    for b in range(GB):
                        last = mm(bank[:, b * D:(b + 1) * D], ctxs[:, (GB * gg + b) * S:(GB * gg + b + 1) * S],
                                  w[:, WV + layer * D:WV + (layer + 1) * D], start=True, stop=True)
                elif kind == "Q":
                    if layer > 0:
                        pe.wait_ge(g_evac, index["X", g] + 1)
                    src = xt[:, tok] if layer == 0 else xg[:, :]
                    last = mm(bank, w[:, WQ + layer * D:WQ + (layer + 1) * D], src, start=True, stop=True)
                elif kind == "X":
                    last = transposed_rows(norm, g, norm_index(source[layer], gg))
                elif kind == "FX":
                    last = transposed_rows(norm, g, norm_index(1, gg))
                elif kind[0] == "H":
                    j = int(kind[1])
                    pe.wait_ge(g_evac, index["FX", g] + 1)
                    last = mm(bank, w[:, W1 + j * 128:W1 + (j + 1) * 128], xg[:, :], start=True, stop=True)
                else:
                    pe.wait_ge(g_evac, index["H3", g] + 1)
                    for b in range(GB):
                        for j in range(4):
                            last = mm(bank[:, b * D:(b + 1) * D], hid[:, j, b * S:(b + 1) * S],
                                      w[:, W2 + j * D:W2 + (j + 1) * D], start=j == 0, stop=j == 3)
                last.then_inc(g_ready, 1)

            for s, i in steps:
                if (s, i) in at:
                    group_task(*at[s, i])
                if 0 <= s + 2 < UNITS:
                    scores(s + 2, i)
                if 0 <= s < UNITS:
                    shifted_scores(s, i)
                n = CH * s + i - 2
                if 0 <= n < CH * UNITS:
                    values(n)
                if i == 1 and 0 <= s + 1 < UNITS:
                    u = s + 1
                    pe.wait_ge(nparts_done, u + 1)
                    if u > 2:
                        pe.wait_ge(onorm_done, u - 2)
                    if u == 0:
                        pe.wait_ge(ident_ready, 1)
                    nc.tensor.transpose(ps[0:48, BK_X, 0:S // 2].bitcast(BF16), nparts[:, :, :].rearrange("p n h -> p (n h)"),
                                        identb[:, :]).then_inc(mt_ready, 1)
                if i == 3 and 0 <= s - 1 < UNITS:
                    u = s - 1
                    pe.wait_ge(o9_evac, u + 1)
                    pe.wait_ge(mt_evac, min(u + 3, UNITS))
                    if u == 0:
                        pe.wait_ge(ld_id, 16)
                    for j in range(CH):
                        last = nc.tensor.transpose(ps[:, BK_X, j * S:(j + 1) * S], o9[:, j, :], ident[:, :])
                    last.then_inc(ox_ready, 1)
                if i == 1 and 0 <= s - 2 < UNITS:
                    u = s - 2
                    pe.wait_ge(onorm_done, u + 1)
                    if u > 0:
                        pe.wait_ge(resid_done, u)
                    nc.tensor.transpose(ps[:, BK_Y, 0:S], onorm[:, :], ident[:, :]).then_inc(ot_ready, 1)
                if i == 3 and 0 <= s - 2 < UNITS:
                    u = s - 2
                    layer = u // B
                    pe.wait_ge(ot_evac, u + 1)
                    mm(ps[:, BK_Y, S:2 * S], onT[:, :], w[:, WO + layer * D:WO + (layer + 1) * D],
                       start=True, stop=True).then_inc(wo_ready, 1)

        @block.scalar
        def _(act):
            def evacuate(kind, g):
                layer, gg, n = g // NG, g % NG, index[kind, g]
                bank = ps[:, BK_G, :]
                if kind in ("Q", "F2"):
                    return
                act.wait_ge(g_ready, n + 1)
                if kind == "A":
                    if g > 0:
                        act.wait_ge(g_evac, index["Q", g - 1] + 1)
                    i_ = nc.scalar.activation(qscale[:, :], bank, ACT.Copy, scale=SCALE)
                elif kind == "K":
                    if g == 0:
                        act.wait_ge(ld_vec, 16)
                    else:
                        act.wait_ge(r1["K"], g)
                    i_ = nc.scalar.activation(full["K"][:, :], bank, ACT.Identity, bias=vec[:, VBK + layer:VBK + layer + 1])
                elif kind == "V":
                    if g >= STACKS:
                        act.wait_ge(pv_done, 4 * CH * (g - STACKS + 1))
                    if g == 0:
                        act.wait_ge(const_ready, 1)
                    i_ = nc.scalar.activation(vst[g % STACKS][:, :, :, 0:DK].rearrange("p b h d -> p (b h) d"),
                                              bank.rearrange("p (n d) -> p n d", d=DK), ACT.Copy)
                elif kind in ("X", "FX"):
                    m = 1 if kind == "FX" else (0 if layer == 1 else 2)
                    i_ = nc.scalar.activation(xg[:, :], bank, ACT.Identity, scale=vec[:, VG + m:VG + m + 1],
                                              bias=vec[:, VB + m:VB + m + 1])
                else:
                    j = int(kind[1])
                    i_ = nc.scalar.activation(hid[:, j, :], bank, ACT.Relu, bias=vec[:, VB1 + j:VB1 + j + 1])
                i_.then_inc(g_evac, 1)

            for s, i in steps:
                if i == 2 and 0 <= s - 1 < UNITS:
                    u = s - 1
                    act.wait_ge(pv_done, CH * (u + 1))
                    if u > 0:
                        act.wait_ge(ox_ready, u)
                    nc.scalar.activation(o9[:, :, :].rearrange("p c q -> p (c q)"), ps[:, BK_PV, :], ACT.Copy).then_inc(o9_evac, 1)
                if 0 <= s < UNITS:
                    n = CH * s + i
                    act.wait_ge(st_ready, n + 1)
                    if n >= PROBS:
                        act.wait_ge(pv_done, n - PROBS + 1)
                    nc.scalar.activation(probs[:, n % PROBS, :, :].rearrange("p h q -> p (h q)"),
                                         ps[:, BK_ST + n % 2, :], ACT.Exp).then_inc(exp_done, 1)
                if (s, i) in at:
                    evacuate(*at[s, i])
                if i == 1 and 0 <= s + 1 < UNITS:
                    u = s + 1
                    act.wait_ge(mt_ready, u + 1)
                    if u >= 2:
                        act.wait_ge(max_loaded[u % 2], 16 * (u // 2))
                    nc.scalar.activation(mt[:, u % 2, :], ps[0:48, BK_X, 0:S // 2].bitcast(BF16), ACT.Copy).then_inc(mt_evac, 1)
                if i == 2 and 0 <= s - 2 < UNITS:
                    u = s - 2
                    act.wait_ge(ot_ready, u + 1)
                    if u > 0:
                        act.wait_ge(wo_ready, u)
                    nc.scalar.activation(onT[:, :], ps[:, BK_Y, 0:S], ACT.Identity,
                                         bias=vec[:, VBV + u // B:VBV + u // B + 1]).then_inc(ot_evac, 1)

        @block.vector
        def _(dve):
            v = nc.vector
            v.memset(kst[0][:, :, :, :].rearrange("p n a t -> p (n a t)").bitcast(U32), 0).then_inc(zeroed[0], 1)
            v.memset(qst[0][:, :, :].rearrange("p n t -> p (n t)").bitcast(U32), 0).then_inc(zeroed[0], 1)
            dve.wait_ge(ld_id, 16)
            v.tensor_copy(identb[:, :], ident[:, :]).then_inc(ident_ready, 1)
            dve.wait_ge(ld_mqk, 16)
            v.tensor_scalar(mqk[:, :, :], mqk_in, 0.0, NEG, ALU.is_equal, ALU.mult).then_inc(masks_ready, 1)
            dve.wait_ge(masks_ready, 1)
            v.tensor_reduce(anyf[:, :], mqk[:, :, :], AX.X, ALU.max).then_inc(mask_step, 1)
            dve.wait_ge(mask_step, 1)
            v.tensor_scalar(anyk[:, :], anyf[:, :], 0.0, None, ALU.is_ge).then_inc(mask_step, 1)

            def key_mask():
                dve.wait_ge(ld_mk, 16)
                v.tensor_scalar(mk[:, :, :], mk_in, 0.0, NEG, ALU.is_equal, ALU.mult).then_inc(bias_rows, 1)
                dve.wait_ge(bias_rows, 1)
                dve.wait_ge(mask_step, 2)
                v.tensor_reduce(anyf[:, :], mk[:, :, :], AX.X, ALU.max).then_inc(mask_step, 1)
                dve.wait_ge(mask_step, 3)
                v.tensor_scalar(cscale[:, :], anyf[:, :], 0.0, SCALE, ALU.is_ge, ALU.mult).then_inc(mask_step, 1)

            def normalize(n, sums, stats, group):
                dve.wait_ge(rstd_done, n + 1)
                for b in range(GB):
                    last = v.tensor_scalar(norm[:, GB * group + b, :], sums[:, b, :], stats[:, b, 0:1],
                                           rstd[:, n % 2, b:b + 1], ALU.subtract, ALU.mult)
                last.then_inc(norm_done, 1)

            def first_part(m, g):
                if m == "K":
                    dve.wait_ge(g_evac, index["K", g] + 1)
                else:
                    dve.wait_ge(g_evac, index["Q", g] + 1)
                if g > 0:
                    dve.wait_ge(stacked[(g - 1) % STACKS], all_stacked(g - 1))
                v.tensor_copy(part[m][:, 0, :], full[m][:, :]).then_inc(p1[m], 1)

            def second_part(m, g):
                dve.wait_ge(r1[m], g + 1)
                v.tensor_copy(part[m][:, 1, :], rest[m][:, :]).then_inc(p2[m], 1)

            for s, i in steps:
                if 0 <= s + 2 < UNITS:
                    u = s + 2
                    n = CH * u + i
                    dve.wait_ge(s_ready, n + 1)
                    if i == 0 and u >= 2:
                        dve.wait_ge(nparts_done, u - 1)
                    v.tensor_reduce(negm[:, u % 2, 4 * i:4 * i + 4], ps[:, BK_S + n % 2, :].rearrange("p (h k) -> p h k", h=4),
                                    AX.X, ALU.max, negate=True).then_inc(max_done, 1)
                if i == 0 and 0 <= s - 2 < UNITS:
                    u = s - 2
                    view = ps[:, BK_X, :].rearrange("p (h e) -> p h e", e=32)
                    dve.wait_ge(ox_ready, u + 1)
                    v.reciprocal(rec[:, :].unsqueeze(2), view[:, :, DK:DK + 1]).then_inc(rec_done, 1)
                    dve.wait_ge(rec_done, u + 1)
                    if u > 0:
                        dve.wait_ge(ot_ready, u)
                    v.tensor_tensor(onorm[:, :].rearrange("p (h d) -> p h d", d=DK), view[:, :, 0:DK],
                                    rec[:, :].unsqueeze(2).to_broadcast([128, H, DK]), ALU.mult).then_inc(onorm_done, 1)
                if i == 0 and 0 <= s - 3 < UNITS:
                    u = s - 3
                    g, b = u // 4, u % 4
                    dve.wait_ge(wo_ready, u + 1)
                    if b == 0:
                        dve.wait_ge(res_done, res_order.index((u // B, g % NG)) + 1)
                    v.tensor_tensor(rsum[:, 0, b, :], ps[:, BK_Y, S:2 * S], res[:, GB * (g % NG) + b, :], ALU.add)\
                        .then_inc(resid_done, 1)
                    dve.wait_ge(resid_done, u + 1)
                    v.bn_stats(stat[:, b, :], rsum[:, 0, b, :]).then_inc(stat_done, 1)
                    dve.wait_ge(stat_done, u + 1)
                    v.bn_aggr(mv[:, b, :], stat[:, b, :]).then_inc(mv_done, 1)
                if i == 2 and 0 <= s - 3 < UNITS and (s - 3) % 4 == 3:
                    u = s - 3
                    layer, gg = u // B, (u // 4) % NG
                    dve.wait_ge(mv_done, u + 1)
                    if layer == 0 and gg == 0:
                        dve.wait_ge(masks_ready, 1)
                    if layer > 0:
                        before = ("F" if layer == 2 else layer - 1, gg)
                        dve.wait_ge(gain_done, norm_order.index(before) + 2)
                    normalize(norm_index(layer, gg), rsum[:, 0, :, :], mv, gg)
                kind, g = at.get((s, i), ("", 0))
                if kind == "Q":
                    layer = g // NG
                    dve.wait_ge(g_ready, index["Q", g] + 1)
                    if g > 0:
                        dve.wait_ge(r1["Q"], g)
                    bank = ps[:, BK_G, :]
                    bias = vec[:, VBQ + layer:VBQ + layer + 1]
                    if g == 0:
                        dve.wait_ge(ld_vec, 16)
                    if layer == 0:
                        dve.wait_ge(g_evac, index["A", g] + 1)
                        i_ = v.scalar_tensor_tensor(full["Q"][:, :], bank, bias, qscale[:, :], ALU.add, ALU.mult)
                    elif layer == 1:
                        if g == NG:
                            dve.wait_ge(mask_step, 4)
                        i_ = v.scalar_tensor_tensor(
                            full["Q"][:, :].rearrange("p (b t) -> p b t", b=GB), bank.rearrange("p (b t) -> p b t", b=GB), bias,
                            cscale[:, GB * (g % NG):GB * (g % NG) + GB].unsqueeze(2).to_broadcast([128, GB, S]), ALU.add, ALU.mult)
                    else:
                        i_ = v.tensor_scalar(full["Q"][:, :], bank, bias, SCALE, ALU.add, ALU.mult)
                    i_.then_inc(g_evac, 1)
                if kind == "F2":
                    gg, n = g % NG, g - 2 * NG
                    dve.wait_ge(g_ready, index["F2", g] + 1)
                    dve.wait_ge(res_done, res_order.index(("F", gg)) + 1)
                    v.tensor_tensor(rsum[:, 1, :, :].rearrange("p b d -> p (b d)"), ps[:, BK_G, :],
                                    res[:, GB * gg:GB * gg + GB, :].rearrange("p b d -> p (b d)"), ALU.add).then_inc(g_evac, 1)
                    dve.wait_ge(g_evac, index["F2", g] + 1)
                    for b in range(GB):
                        last = v.bn_stats(fstat[:, b, :], rsum[:, 1, b, :])
                    last.then_inc(fstat_done, 1)
                    dve.wait_ge(fstat_done, n + 1)
                    for b in range(GB):
                        last = v.bn_aggr(fmv[:, b, :], fstat[:, b, :])
                    last.then_inc(fmv_done, 1)
                if i == 3 and at.get((s, 1), ("", 0))[0] == "F2":
                    g = at[s, 1][1]
                    dve.wait_ge(gain_done, norm_index(1, g % NG) + 2)
                    dve.wait_ge(fmv_done, g - 2 * NG + 1)
                    normalize(norm_index("F", g % NG), rsum[:, 1, :, :], fmv, g % NG)
                for m, slot, step, do in (("K", 8, 3, first_part), ("K", 7, 1, second_part),
                                          ("Q", 6, 0, first_part), ("Q", 6, 2, second_part)):
                    if i == step and (s + slot) % 4 == 0 and 0 <= (s + slot) // 4 < GROUPS:
                        do(m, (s + slot) // 4)
                if s == -1 and i == 0:
                    key_mask()

        @block.gpsimd
        def _(pool):
            gp = nc.gpsimd
            for n in range(STACKS):
                last = gp.memset(vst[n][:, :, :, DK:32].rearrange("p b h d -> p (b h) d"), 1.0)
                if n == 0:
                    gp.memset(mhalf[:, :], -0.5)
                    gp.memset(zrow[:, :], 0.0)
                if n > 0:
                    gp.memset(kst[n][:, :, :, :].rearrange("p n a t -> p (n a t)").bitcast(U32), 0).then_inc(zeroed[n], 1)
                    gp.memset(qst[n][:, :, :].rearrange("p n t -> p (n t)").bitcast(U32), 0).then_inc(zeroed[n], 1)
            last.then_inc(const_ready, 1)

            def gain_row(j):
                return row[:, R_G + j, :].unsqueeze(1).to_broadcast([128, GB, D])

            def offset_row(j):
                return row[:, R_B + j, :].unsqueeze(1).to_broadcast([128, GB, D])

            pool.wait_ge(ld_row, 16)
            for j in range(3):
                last = gp.tensor_tensor(row[:, R_B + j, :], row[:, R_B + j, :], row[:, R_BO + j, :], ALU.add)
            last.then_inc(gain_done, 1)
            pool.wait_ge(ld_res, 16)
            for g in range(NG):
                gp.tensor_tensor(res[:, GB * g:GB * g + GB, :], res[:, GB * g:GB * g + GB, :],
                                 row[:, R_BOSA, :].unsqueeze(1).to_broadcast([128, GB, D]), ALU.add).then_inc(res_done, 1)

            def deviation(n, stats):
                if n > 1:
                    pool.wait_ge(norm_done, n - 1)
                gp.tensor_scalar(vareps[:, n % 2, :].unsqueeze(2), stats[:, :, 1:2], EPS, None, ALU.add).then_inc(vareps_done, 1)
                pool.wait_ge(vareps_done, n + 1)
                gp.tensor_tensor(rstd[:, n % 2, :], vareps[:, n % 2, :], mhalf[:, :], ALU.pow).then_inc(rstd_done, 1)

            def affine(n, layer, gg):
                j = {0: 0, 1: 1, "F": 2, 2: 3}[layer]
                pool.wait_ge(norm_done, n + 1)
                if layer == 2:
                    dst = fin[:, gg % 2, :, :]
                    if gg >= 2:
                        pool.wait_ge(stored[gg % 2], 16 * (gg // 2))
                else:
                    dst = res[:, GB * gg:GB * gg + GB, :]
                gp.tensor_tensor(dst, norm[:, GB * gg:GB * gg + GB, :], gain_row(j), ALU.mult).then_inc(gain_done, 1)
                pool.wait_ge(gain_done, n + 2)
                gp.tensor_tensor(dst, dst, offset_row(j), ALU.add).then_inc(fin_ready if layer == 2 else res_done, 1)

            for s, i in steps:
                if i == 0 and 0 <= s + 1 < UNITS:
                    u = s + 1
                    heads = negm[:, u % 2, :].rearrange("p (n a) -> p a n", a=2)
                    left = nrest[:, u % 2, :].rearrange("p (a n) -> p a n", a=2)
                    pt = [nparts[:, n, :].rearrange("p (a n) -> p a n", a=2) for n in range(3)]
                    pool.wait_ge(max_done, CH * (u + 1))
                    if u > 0:
                        pool.wait_ge(mt_ready, u)
                    gp.tensor_copy(pt[0], heads).then_inc(nparts_step, 1)
                    pool.wait_ge(nparts_step, 3 * u + 1)
                    gp.tensor_tensor(left, heads, pt[0], ALU.subtract).then_inc(nparts_step, 1)
                    pool.wait_ge(nparts_step, 3 * u + 2)
                    gp.tensor_copy(pt[1], left).then_inc(nparts_step, 1)
                    pool.wait_ge(nparts_step, 3 * u + 3)
                    gp.tensor_tensor(pt[2], left, pt[1], ALU.subtract).then_inc(nparts_done, 1)
                if i == 0 and 0 <= s - 3 < UNITS and (s - 3) % 4 == 3:
                    u = s - 3
                    pool.wait_ge(mv_done, u + 1)
                    deviation(norm_index(u // B, (u // 4) % NG), mv)
                if i == 1 and at.get((s, 1), ("", 0))[0] == "F2":
                    g = at[s, 1][1]
                    pool.wait_ge(fmv_done, g - 2 * NG + 1)
                    deviation(norm_index("F", g % NG), fmv)
                if i == 2 and 0 <= s - 3 < UNITS and (s - 3) % 4 == 3:
                    u = s - 3
                    affine(norm_index(u // B, (u // 4) % NG), u // B, (u // 4) % NG)
                if i == 3 and at.get((s, 1), ("", 0))[0] == "F2":
                    g = at[s, 1][1]
                    affine(norm_index("F", g % NG), "F", g % NG)
                for m, slot, step in (("K", 8, 3), ("Q", 6, 0)):
                    if i == step and (s + slot) % 4 == 0 and 0 <= (s + slot) // 4 < GROUPS:
                        g = (s + slot) // 4
                        pool.wait_ge(p1[m], g + 1)
                        if g > 0:
                            pool.wait_ge(p2[m], g)
                            pool.wait_ge(p3[m], g)
                        gp.tensor_tensor(rest[m][:, :], full[m][:, :], part[m][:, 0, :], ALU.subtract).then_inc(r1[m], 1)
                for m, slot, step in (("K", 7, 1), ("Q", 6, 2)):
                    if i == step and (s + slot) % 4 == 0 and 0 <= (s + slot) // 4 < GROUPS:
                        g = (s + slot) // 4
                        pool.wait_ge(p2[m], g + 1)
                        gp.tensor_tensor(part[m][:, 2, :], rest[m][:, :], part[m][:, 1, :], ALU.subtract).then_inc(p3[m], 1)


def kernel(**inputs):
    import ml_dtypes as _ml
    import numpy as _np
    import concourse.bacc as _bacc
    from concourse import mybir as _mybir
    from concourse.bass_utils import run_bass_kernel_spmd as _run

    a = {k: _np.asarray(v) for k, v in inputs.items()}

    def to_rows(wt):
        return wt.reshape(PAIRS, 2, DK, D).transpose(3, 1, 2, 0).reshape(D, D)

    def to_col(bias):
        return bias.reshape(PAIRS, 2, DK).transpose(1, 2, 0).reshape(D, 1)

    att = [("L0_xattn_sa_w", "L0_xattn_sa_b"), ("L0_xattn_ca_w", "L0_xattn_ca_b"), ("L1_xattn_W", "L1_xattn_b")]
    weights = _np.concatenate(
        [to_rows(a[wn + "q"]) for wn, _ in att] + [to_rows(a[wn + "k"]) for wn, _ in att]
        + [a[wn + "v"].T for wn, _ in att] + [a[wn + "o"].T for wn, _ in att]
        + [a["L0_xattn_ffn_w1"].T]
        + [a["L0_xattn_ffn_w2"].T.reshape(4, 128, D).transpose(1, 0, 2).reshape(128, FF)], axis=1)
    vectors = _np.concatenate(
        [to_col(a[bn + "q"]) for _, bn in att] + [to_col(a[bn + "k"]) for _, bn in att]
        + [a[bn + "v"].reshape(D, 1) for _, bn in att]
        + [a["L0_xattn_ffn_b1"].reshape(4, 128).T]
        + [a[f"L0_xattn_ln{n}_g"].reshape(D, 1) for n in (1, 2, 3)]
        + [a[f"L0_xattn_ln{n}_b"].reshape(D, 1) for n in (1, 2, 3)], axis=1)
    rows = _np.stack(
        [a["L0_xattn_sa_bo"]] + [a[f"L0_xattn_ln{n}_g"] for n in (1, 2, 3)] + [a["L1_xattn_ln_gamma"]]
        + [a[f"L0_xattn_ln{n}_b"] for n in (1, 2, 3)] + [a["L1_xattn_ln_beta"]]
        + [a["L0_xattn_ca_bo"], a["L0_xattn_ffn_b2"], a["L1_xattn_bo"]])
    k_rows = _np.zeros((32, PAIRS, 2, GT), _ml.bfloat16)
    for n in range(3):
        for h in range(2):
            k_rows[1 + 2 * n + h, :, h, :] = 1
    q_rows = _np.zeros((32, PAIRS, GT), _ml.bfloat16)
    q_rows[0] = 1
    arrays = {
        "x_tok": a["x"], "x_t": a["x"].transpose(2, 0, 1).reshape(D, B * S),
        "ctx_t": a["ctx_1024"].transpose(2, 0, 1).reshape(D, B * S),
        "mask_k": a["mask_Bx1x1xS2_if1"].reshape(B, S), "mask_qk": a["mask_Bx1xSxS2_if1"].reshape(B, S, S),
        "weights": weights, "vectors": vectors, "rows": rows, "k_rows": k_rows, "q_rows": q_rows,
        "ident": _np.eye(128, dtype=_np.float32),
    }
    arrays = {k: _np.ascontiguousarray(v) for k, v in arrays.items()}
    nc = _bacc.Bacc("TRN2", target_bir_lowering=False, num_devices=1)
    args = [nc.dram_tensor("in_" + k, v.shape, _mybir.dt.from_np(v.dtype), kind="ExternalInput").ap() for k, v in arrays.items()]
    args.append(nc.dram_tensor("out_0", (B, S, D), _mybir.dt.float32, kind="ExternalOutput").ap())
    build(nc, *args)
    r = _run(nc, [{"in_" + k: v for k, v in arrays.items()}], core_ids=[0])
    return r.results[0]["out_0"]
```

```python
import concourse.bass as bass
from concourse import mybir
from contextlib import ExitStack

F32 = mybir.dt.float32
BF16 = mybir.dt.bfloat16
I32 = mybir.dt.int32
U32 = mybir.dt.uint32
ALU = mybir.AluOpType
ACT = mybir.ActivationFunctionType
AX = mybir.AxisListType

B, S, D, H, DK, FF = 16, 128, 128, 16, 8, 512
PAIRS = H // 2
LAYERS = 3
GB = 4
GT = GB * S
NG = B // GB
UNITS, GROUPS = LAYERS * B, LAYERS * NG
CH = H // 4
NPROD = 6
Q_PART = [0, 0, 0, 1, 1, 2]
K_PART = [0, 1, 2, 0, 1, 0]
MASK_ROW = 16 * NPROD
MAX_ROW = MASK_ROW + 1
K_SCORES = MAX_ROW
K_SHIFTED = MAX_ROW + 6
SCALE = float(1.0 / DK ** 0.5)
NEG = -float(2 ** 30)
EPS = 1e-5
STACKS = 3
TWO_ONES = 1.0 + 0x3F80 / 2 ** 23
PROBS = 6
LEAD = 3

WQ, WK, WV, WO, WL = 0, D, 2 * D, 3 * D, 4 * D
W1, W2 = LAYERS * WL, LAYERS * WL + FF
WCOLS = W2 + FF
VBQ, VBK, VBV, VB1, VG, VB = 0, 3, 6, 9, 13, 16
VCOLS = 19
R_BOSA, R_G, R_B, R_BO = 0, 1, 5, 9
ROWS = 12
BK_S, BK_ST, BK_PV, BK_X, BK_G, BK_Y = 0, 2, 4, 5, 6, 7


def schedule():
    tasks = []
    for g in range(GROUPS):
        s = 4 * g
        if g == 0:
            tasks += [(s - 8, 3, "K", g), (s - 7, 0, "A", g), (s - 6, 1, "Q", g), (s - 6, 2, "V", g)]
        elif g == 1:
            tasks += [(s - 9, 2, "K", g), (s - 9, 3, "V", g), (s - 8, 0, "A", g), (s - 8, 1, "Q", g)]
        elif g < NG:
            tasks += [(s - 8, 3, "K", g), (s - 7, 1, "A", g), (s - 7, 3, "Q", g), (s - 6, 2, "V", g)]
        else:
            tasks += [(s - 8, 3, "K", g), (s - 7, 2, "X", g), (s - 7, 3, "Q", g), (s - 6, 2, "V", g)]
        if g >= 2 * NG:
            tasks += [(s - 9, 0, "FX", g), (s - 9, 1, "H0", g), (s - 9, 2, "H1", g), (s - 9, 3, "H2", g),
                      (s - 8, 0, "H3", g), (s - 8, 2, "F2", g)]
    return sorted(tasks)


def build(nc, x_tok, x_t, ctx_t, mask_k, mask_qk, weights, vectors, rows, k_rows, ident_in, out):
    tasks = schedule()
    index = {(kind, g): n for n, (_, _, kind, g) in enumerate(tasks)}
    at = {(slot, step): (kind, g) for slot, step, kind, g in tasks}
    first_slot, last_slot = -8, UNITS + 4
    steps = [(s, i) for s in range(first_slot, last_slot + 1) for i in range(CH)]

    def group_of(s, lead, first=0):
        g = (s + lead) // 4
        return g if (s + lead) % 4 == 0 and first <= g < GROUPS else None

    def attention_end(s):
        u = s - 3
        return u // 4 if 0 <= u < UNITS and u % 4 == 3 else None

    ctx = ExitStack()
    with ctx:
        def sb(name, shape, dt=F32):
            return ctx.enter_context(nc.sbuf_tensor(name, shape, dt))

        def sem(name):
            return ctx.enter_context(nc.semaphore(name))

        w = sb("w", [128, WCOLS])
        vec = sb("vec", [128, VCOLS])
        row = sb("row", [128, ROWS, D])
        ident = sb("ident", [128, 128])
        identb = sb("identb", [128, 128], BF16)
        xt = sb("xt", [128, B * S])
        ct = sb("ct", [128, B * S])
        res = sb("res", [128, B, D])
        norm = sb("norm", [128, B, D])
        rsum = sb("rsum", [128, 3, GB, D])
        stat = sb("stat", [128, GB, 6])
        mv = sb("mv", [128, 2, GB, 2])
        fstat = sb("fstat", [128, GB, 6])
        fmv = sb("fmv", [128, GB, 2])
        rstd = sb("rstd", [128, 2, GB])
        vareps = sb("vareps", [128, 2, GB])
        mhalf = sb("mhalf", [128, GB])
        xg = sb("xg", [128, GT])
        hid = sb("hid", [128, 4, GT])
        qst = [sb(f"qst{n}", [128, PAIRS, GT], BF16) for n in range(STACKS)]
        kst = [sb(f"kst{n}", [128, PAIRS, 2, GT], BF16) for n in range(STACKS)]
        vst = [sb(f"vst{n}", [128, GB, H, 32]) for n in range(STACKS)]
        full = {m: sb(f"full{m}", [128, GT]) for m in "QK"}
        rest = {m: sb(f"rest{m}", [128, GT]) for m in "QK"}
        part = {m: sb(f"part{m}", [128, 3, GT], BF16) for m in "QK"}
        probs = sb("probs", [128, PROBS, 4, S])
        qscale = sb("qscale", [128, GT])
        cscale = sb("cscale", [128, B])
        anyk = sb("anyk", [128, B], BF16)
        anyf = sb("anyf", [128, B])
        mqk = sb("mqk", [128, B, S], BF16)
        mk = sb("mk", [128, B, S], BF16)
        zrow = sb("zrow", [1, GT], BF16)
        negm = sb("negm", [128, LEAD, H])
        nrest = sb("nrest", [128, 2, H])
        nparts = sb("nparts", [128, 2, 3, H], BF16)
        mt = sb("mt", [48, 2, S], BF16)
        o9 = sb("o9", [128, CH, S])
        rec = sb("rec", [128, H])
        onorm = sb("onorm", [128, D])
        onT = sb("onT", [128, S])
        fin = sb("fin", [128, 2, GB, D])
        ps = ctx.enter_context(nc.psum_tensor("ps", [128, 8, 512], F32))
        mqk_in = norm[:, :, :].bitcast(I32)
        mk_in = hid[:, :, :].bitcast(I32).rearrange("p a (b k) -> p (a b) k", k=S)

        ld_w, ld_w2, ld_x2, ld_vec, ld_row, ld_id = sem("ld_w"), sem("ld_w2"), sem("ld_x2"), sem("ld_vec"), sem("ld_row"), sem("ld_id")
        ld_x, ld_c, ld_res, ld_mk = sem("ld_x"), [sem(f"ld_c{g}") for g in range(NG)], [sem(f"ld_res{g}") for g in range(NG)], sem("ld_mk")
        ld_mqk = [sem(f"ld_mqk{g}") for g in range(NG)]
        zeroed = [sem(f"zeroed{n}") for n in range(STACKS)]
        q_ones = [sem(f"q_ones{n}") for n in range(STACKS)]
        ld_rows = [sem(f"ld_rows{n}") for n in range(STACKS)]
        k_stacked = [sem(f"k_stacked{n}") for n in range(STACKS)]
        q_stacked = [sem(f"q_stacked{n}") for n in range(STACKS)]
        ident_ready, const_ready, masks_ready = sem("ident_ready"), sem("const_ready"), sem("masks_ready")
        mask_step, flags_ready, bias_rows = sem("mask_step"), sem("flags_ready"), sem("bias_rows")
        g_ready, g_evac = sem("g_ready"), sem("g_evac")
        s_ready, max_done = sem("s_ready"), sem("max_done")
        nparts_step, nparts_done, mt_ready, mt_evac = sem("nparts_step"), sem("nparts_done"), sem("mt_ready"), sem("mt_evac")
        max_loaded = [sem("max_loaded0"), sem("max_loaded1")]
        st_ready, exp_done, pv_done, o9_evac = sem("st_ready"), sem("exp_done"), sem("pv_done"), sem("o9_evac")
        ox_ready, rec_done, onorm_done, ot_ready, ot_evac = (
            sem("ox_ready"), sem("rec_done"), sem("onorm_done"), sem("ot_ready"), sem("ot_evac"))
        wo_ready, resid_done, stat_done, mv_done = sem("wo_ready"), sem("resid_done"), sem("stat_done"), sem("mv_done")
        fres_done, fstat_done, fmv_done = sem("fres_done"), sem("fstat_done"), sem("fmv_done")
        vareps_done, rstd_done, norm_done, gain_done, res_done = (
            sem("vareps_done"), sem("rstd_done"), sem("norm_done"), sem("gain_done"), sem("res_done"))
        p1 = {m: sem(f"part1_{m}") for m in "QK"}
        r1 = {m: sem(f"rest_{m}") for m in "QK"}
        p2 = {m: sem(f"part2_{m}") for m in "QK"}
        p3 = {m: sem(f"part3_{m}") for m in "QK"}
        fin_ready, stored = sem("fin_ready"), [sem("stored0"), sem("stored1")]

        def mask_dma(g):
            return NG <= g < 2 * NG or 2 * NG <= g < 2 * NG + STACKS

        def k_dmas(g):
            return 16 * sum(2 * NPROD + (1 if mask_dma(o) else 0) for o in range(g % STACKS, g + 1, STACKS))

        def q_dmas(g):
            return 16 * NPROD * (g // STACKS + 1)

        def norm_index(layer, g):
            return norm_order.index((layer, g))

        norm_order = []
        for s, i in steps:
            g = attention_end(s)
            if i == 3 and g is not None:
                norm_order.append((g // NG, g % NG))
            g = group_of(s, 7, 2 * NG)
            if i == 1 and g is not None:
                norm_order.append(("F", g % NG))
        res_order = [(0, g) for g in range(NG)]
        for layer, g in norm_order:
            if layer != 2:
                res_order.append(({0: 1, 1: "F", "F": 2}[layer], g))
        source = {1: 0, 2: "F"}

        block = ctx.enter_context(nc.Block())

        @block.sync
        def _(sp):
            sp.dma_start(w[:, 0:WL], weights[:, 0:WL]).then_inc(ld_w, 16)
            sp.dma_start(xt[:, 0:GT], x_t[:, 0:GT]).then_inc(ld_x, 16)
            sp.dma_start(vec[:, :], vectors).then_inc(ld_vec, 16)
            sp.dma_start(ident[:, :], ident_in).then_inc(ld_id, 16)

            def query_mask(g):
                sp.dma_start(mqk_in[:, GB * g:GB * g + GB, :], mask_qk[GB * g:GB * g + GB].rearrange("b q k -> q b k"))\
                    .then_inc(ld_mqk[g], 16)

            def max_rows(n):
                sp.wait_ge(zeroed[n], 1)
                sp.dma_start(kst[n][MAX_ROW:K_SHIFTED, :, :, :], k_rows).then_inc(ld_rows[n], 16)

            query_mask(0)
            max_rows(0)
            sp.dma_start(xt[:, GT:B * S], x_t[:, GT:B * S]).then_inc(ld_x2, 16)
            query_mask(1)

            def row_load():
                sp.dma_start(row[:, :, :], rows.partition_broadcast(128)).then_inc(ld_row, 16)

            def residual_load(g):
                sp.dma_start(res[:, GB * g:GB * g + GB, :], x_tok[GB * g:GB * g + GB].rearrange("b t d -> t b d")).then_inc(ld_res[g], 16)

            def context_load(g):
                sp.dma_start(ct[:, GT * g:GT * g + GT], ctx_t[:, GT * g:GT * g + GT]).then_inc(ld_c[g], 16)

            def key_mask_load():
                sp.dma_start(mk_in, mask_k.partition_broadcast(128)).then_inc(ld_mk, 16)

            def weight_load():
                sp.dma_start(w[:, WL:WCOLS], weights[:, WL:WCOLS]).then_inc(ld_w2, 16)

            LOADS = {(-5, 3): lambda: max_rows(1), (-2, 0): lambda: query_mask(2), (-1, 3): row_load, (0, 0): lambda: query_mask(3),
                     (0, 1): lambda: residual_load(0), (1, 1): lambda: residual_load(1),
                     (1, 0): lambda: max_rows(2), (2, 1): lambda: residual_load(2), (3, 1): lambda: residual_load(3),
                     (4, 1): key_mask_load, (5, 1): weight_load, (6, 1): lambda: context_load(0), (7, 1): lambda: context_load(1),
                     (8, 1): lambda: context_load(2), (9, 1): lambda: context_load(3)}

            def stack_free(g):
                if g >= STACKS:
                    sp.wait_ge(st_ready, 4 * CH * (g - STACKS + 1))
                else:
                    sp.wait_ge(ld_rows[g], 16)

            def stack_k(g, c):
                for a in range(2):
                    sp.dma_start(kst[g % STACKS][16 * c + 8 * a:16 * c + 8 * a + 8, :, a, :],
                                 part["K"][64 * a:64 * a + 64, K_PART[c], :]).then_inc(k_stacked[g % STACKS], 16)

            def stack_q(g, c):
                sp.dma_start(qst[g % STACKS][16 * c:16 * c + 16, :, :],
                             part["Q"][:, Q_PART[c], :]).then_inc(q_stacked[g % STACKS], 16)

            for s, i in steps:
                if i == 3 and 0 <= s + 2 < UNITS:
                    u = s + 2
                    g, b = u // 4, u % 4
                    sp.wait_ge(mt_evac, u + 1)
                    sp.dma_start(qst[g % STACKS][MAX_ROW:MAX_ROW + 6, :, b * S:(b + 1) * S],
                                 mt[:, u % 2, :]).then_inc(max_loaded[u % 2], 16)
                for n, slot, step in ((0, 7, 2), (1, 6, 1), (2, 6, 3)):
                    g = group_of(s, slot)
                    if i == step and g is not None:
                        if n == 0:
                            stack_free(g)
                            if g < STACKS:
                                sp.wait_ge(q_ones[g], 1)
                        sp.wait_ge((p1["K"], p2["K"], p3["K"])[n], g + 1)
                        for c in range(NPROD):
                            if K_PART[c] == n:
                                stack_k(g, c)
                        if n == 0 and mask_dma(g):
                            src = zrow[0:1, :]
                            if g < 2 * NG:
                                sp.wait_ge(bias_rows, 1)
                                src = mk[0:1, :, :].rearrange("p b k -> p (b k)")[:, (g % NG) * GT:(g % NG + 1) * GT]
                            sp.dma_start(kst[g % STACKS][MASK_ROW:MASK_ROW + 1, :, :, :].rearrange("o p a t -> o (p a) t"),
                                         src.unsqueeze(1).to_broadcast([1, 2 * PAIRS, GT])).then_inc(k_stacked[g % STACKS], 16)
                for n, slot, step in ((0, 6, 2), (1, 5, 1), (2, 5, 3)):
                    g = group_of(s, slot)
                    if i == step and g is not None:
                        sp.wait_ge((p1["Q"], p2["Q"], p3["Q"])[n], g + 1)
                        for c in range(NPROD):
                            if Q_PART[c] == n:
                                stack_q(g, c)
                if (s, i) in LOADS:
                    LOADS[s, i]()
                if i == 2 and attention_end(s - 1) is not None and attention_end(s - 1) >= 2 * NG:
                    g = attention_end(s - 1) - 2 * NG
                    sp.wait_ge(fin_ready, g + 1)
                    sp.dma_start(out[GB * g:GB * g + GB].rearrange("b t d -> t b d"),
                                 fin[:, g % 2, :, :]).then_inc(stored[g % 2], 16)
            sp.wait_ge(stored[0], 16 * (NG // 2))
            sp.wait_ge(stored[1], 16 * (NG // 2))

        @block.tensor
        def _(pe):
            mm = nc.tensor.matmul

            def scores(u, i):
                g, b, n = u // 4, u % 4, CH * u + i
                q, k, tok = qst[g % STACKS], kst[g % STACKS], slice(b * S, (b + 1) * S)
                if b == 0 and i == 0:
                    pe.wait_ge(k_stacked[g % STACKS], k_dmas(g))
                    pe.wait_ge(q_stacked[g % STACKS], q_dmas(g))
                    if g < STACKS:
                        pe.wait_ge(ld_rows[g], 16)
                if n >= 2:
                    pe.wait_ge(max_done, n - 1)
                bank = ps[:, BK_S + n % 2, :]
                masked = u < B
                if masked:
                    if b == 0 and i == 0:
                        pe.wait_ge(masks_ready, g + 1)
                    mm(bank.rearrange("p (h k) -> p h k", h=4), identb[:, :],
                       mqk[:, u, :].unsqueeze(1).to_broadcast([128, 4, S]), start=True, stop=False, skip_group_check=True)
                for j in range(2):
                    p = 2 * i + j
                    last = mm(bank[:, 256 * j:256 * j + 256].rearrange("p (a k) -> p a k", a=2), q[0:K_SCORES, p, tok],
                              k[0:K_SCORES, p, :, tok], start=not masked, stop=True, skip_group_check=True)
                last.then_inc(s_ready, 1)

            def shifted_scores(u, i):
                g, b, n = u // 4, u % 4, CH * u + i
                q, k, tok = qst[g % STACKS], kst[g % STACKS], slice(b * S, (b + 1) * S)
                if i == 0:
                    pe.wait_ge(max_loaded[u % 2], 16 * (u // 2 + 1))
                if n >= 2:
                    pe.wait_ge(exp_done, n - 1)
                bank = ps[:, BK_ST + n % 2, :]
                masked = u < B
                if masked:
                    mm(bank.rearrange("p (h q) -> p h q", h=4), mqk[:, u, :],
                       identb[:, :].unsqueeze(1).to_broadcast([128, 4, S]), start=True, stop=False, skip_group_check=True)
                for c in range(4):
                    p, a = 2 * i + c // 2, c % 2
                    last = mm(bank[:, c * S:(c + 1) * S], k[0:K_SHIFTED, p, a, tok], q[0:K_SHIFTED, p, tok],
                              start=not masked, stop=True, skip_group_check=True)
                last.then_inc(st_ready, 1)

            def values(n):
                u, i = n // CH, n % CH
                g, b = u // 4, u % 4
                pe.wait_ge(exp_done, n + 1)
                if i == 0:
                    if b == 0:
                        pe.wait_ge(g_evac, index["V", g] + 1)
                    if u > 0:
                        pe.wait_ge(o9_evac, u)
                    else:
                        pe.wait_ge(const_ready, 1)
                for c in range(4):
                    last = mm(ps[32 * c:32 * c + 32, BK_PV, i * S:(i + 1) * S], vst[g % STACKS][:, b, 4 * i + c, :],
                              probs[:, n % PROBS, c, :], start=True, stop=True, tile_position=(0, 32 * c))
                last.then_inc(pv_done, 1)

            def transposed_rows(source_rows, g, n):
                pe.wait_ge(norm_done, n + 1)
                for b in range(GB):
                    last = nc.tensor.transpose(ps[:, BK_G, b * S:(b + 1) * S], source_rows[:, GB * (g % NG) + b, :], ident[:, :])
                return last

            def group_task(kind, g):
                layer, gg = g // NG, g % NG
                n = index[kind, g]
                if n > 0:
                    pe.wait_ge(g_evac, n)
                bank = ps[:, BK_G, :]
                ctxs = xt if layer == 0 else ct
                tok = slice(gg * GT, (gg + 1) * GT)
                if kind == "K" and g == 1:
                    pe.wait_ge(ld_x2, 16)
                if kind == "K" and NG <= g < 2 * NG:
                    pe.wait_ge(ld_c[gg], 16)
                if kind == "K" and g == NG:
                    pe.wait_ge(ld_w2, 16)
                if kind == "A":
                    pe.wait_ge(flags_ready, gg + 1)
                    pe.wait_ge(ident_ready, 1)
                    for b in range(GB):
                        last = mm(bank[:, b * S:(b + 1) * S], anyk[:, GB * gg + b:GB * gg + b + 1].to_broadcast([128, 128]),
                                  identb[:, :], start=True, stop=True)
                elif kind == "K":
                    if g == 0:
                        pe.wait_ge(ld_w, 16)
                        pe.wait_ge(ld_x, 16)
                    last = mm(bank, w[:, layer * WL + WK:layer * WL + WK + D], ctxs[:, tok], start=True, stop=True)
                elif kind == "V":
                    for b in range(GB):
                        last = mm(bank[:, b * D:(b + 1) * D], ctxs[:, (GB * gg + b) * S:(GB * gg + b + 1) * S],
                                  w[:, layer * WL + WV:layer * WL + WV + D], start=True, stop=True)
                elif kind == "Q":
                    if layer > 0:
                        pe.wait_ge(g_evac, index["X", g] + 1)
                    src = xt[:, tok] if layer == 0 else xg[:, :]
                    last = mm(bank, w[:, layer * WL + WQ:layer * WL + WQ + D], src, start=True, stop=True)
                elif kind == "X":
                    last = transposed_rows(norm, g, norm_index(source[layer], gg))
                elif kind == "FX":
                    last = transposed_rows(norm, g, norm_index(1, gg))
                elif kind[0] == "H":
                    j = int(kind[1])
                    pe.wait_ge(g_evac, index["FX", g] + 1)
                    last = mm(bank, w[:, W1 + j * 128:W1 + (j + 1) * 128], xg[:, :], start=True, stop=True)
                else:
                    for b in range(GB // 2, GB):
                        for j in range(4):
                            last = mm(bank[:, b * D:(b + 1) * D], hid[:, j, b * S:(b + 1) * S],
                                      w[:, W2 + j * D:W2 + (j + 1) * D], start=j == 0, stop=j == 3)
                last.then_inc(g_ready, 1)

            for s, i in steps:
                if 0 <= s + LEAD < UNITS:
                    scores(s + LEAD, i)
                if 0 <= s < UNITS:
                    shifted_scores(s, i)
                n = CH * s + i - 2
                if i != 2 and 0 <= n < CH * UNITS:
                    values(n)
                if i == 2 and 0 <= s + 2 < UNITS:
                    u = s + 2
                    pe.wait_ge(nparts_done, u + 1)
                    if u > 3:
                        pe.wait_ge(onorm_done, u - 3)
                    elif u > 0:
                        pe.wait_ge(mt_evac, u)
                    if u == 0:
                        pe.wait_ge(ident_ready, 1)
                    nc.tensor.transpose(ps[0:48, BK_X, 0:S // 2].bitcast(BF16), nparts[:, u % 2, :, :].rearrange("p n h -> p (n h)"),
                                        identb[:, :]).then_inc(mt_ready, 1)
                if i == 3 and 0 <= s - 1 < UNITS:
                    u = s - 1
                    pe.wait_ge(o9_evac, u + 1)
                    pe.wait_ge(mt_evac, min(u + 4, UNITS))
                    if u == 0:
                        pe.wait_ge(ld_id, 16)
                    for j in range(CH):
                        last = nc.tensor.transpose(ps[:, BK_X, j * S:(j + 1) * S], o9[:, j, :], ident[:, :])
                    last.then_inc(ox_ready, 1)
                if i == 2 and 0 <= s - 2 < UNITS:
                    u = s - 2
                    pe.wait_ge(onorm_done, u + 1)
                    if u > 0:
                        pe.wait_ge(resid_done, u)
                    nc.tensor.transpose(ps[:, BK_Y, 0:S], onorm[:, :], ident[:, :]).then_inc(ot_ready, 1)
                if i == 2 and 0 <= n < CH * UNITS:
                    values(n)
                if i == 3 and 0 <= s - 2 < UNITS:
                    u = s - 2
                    layer = u // B
                    pe.wait_ge(ot_evac, u + 1)
                    mm(ps[:, BK_Y, S:2 * S], onT[:, :], w[:, layer * WL + WO:layer * WL + WO + D],
                       start=True, stop=True).then_inc(wo_ready, 1)
                if i == 1 and group_of(s, 8, 2 * NG) is not None:
                    g = group_of(s, 8, 2 * NG)
                    pe.wait_ge(g_evac, index["H3", g] + 1)
                    for b in range(GB // 2):
                        for j in range(4):
                            mm(ps[:, BK_G, b * D:(b + 1) * D], hid[:, j, b * S:(b + 1) * S],
                               w[:, W2 + j * D:W2 + (j + 1) * D], start=j == 0, stop=j == 3)
                if (s, i) in at:
                    group_task(*at[s, i])

        @block.scalar
        def _(act):
            def evacuate(kind, g):
                layer, gg, n = g // NG, g % NG, index[kind, g]
                bank = ps[:, BK_G, :]
                if kind in ("Q", "F2"):
                    return
                act.wait_ge(g_ready, n + 1)
                if kind == "A":
                    if g > 0:
                        act.wait_ge(g_evac, index["Q", g - 1] + 1)
                    i_ = nc.scalar.activation(qscale[:, :], bank, ACT.Copy, scale=SCALE)
                elif kind == "K":
                    if g == 0:
                        act.wait_ge(ld_vec, 16)
                    else:
                        act.wait_ge(r1["K"], g)
                    i_ = nc.scalar.activation(full["K"][:, :], bank, ACT.Identity, bias=vec[:, VBK + layer:VBK + layer + 1])
                elif kind == "V":
                    if g >= STACKS:
                        act.wait_ge(pv_done, 4 * CH * (g - STACKS + 1))
                    if g < STACKS:
                        act.wait_ge(const_ready, g + 1)
                    i_ = nc.scalar.activation(vst[g % STACKS][:, :, :, 0:DK].rearrange("p b h d -> p (b h) d"),
                                              bank.rearrange("p (n d) -> p n d", d=DK), ACT.Copy)
                elif kind in ("X", "FX"):
                    m = 1 if kind == "FX" else (0 if layer == 1 else 2)
                    i_ = nc.scalar.activation(xg[:, :], bank, ACT.Identity, scale=vec[:, VG + m:VG + m + 1],
                                              bias=vec[:, VB + m:VB + m + 1])
                else:
                    j = int(kind[1])
                    i_ = nc.scalar.activation(hid[:, j, :], bank, ACT.Relu, bias=vec[:, VB1 + j:VB1 + j + 1])
                i_.then_inc(g_evac, 1)

            for s, i in steps:
                if 0 <= s < UNITS:
                    n = CH * s + i
                    act.wait_ge(st_ready, n + 1)
                    if n >= PROBS:
                        act.wait_ge(pv_done, n - PROBS + 1)
                    nc.scalar.activation(probs[:, n % PROBS, :, :].rearrange("p h q -> p (h q)"),
                                         ps[:, BK_ST + n % 2, :], ACT.Exp).then_inc(exp_done, 1)
                if i == 1 and 0 <= s - 1 < UNITS:
                    u = s - 1
                    act.wait_ge(pv_done, CH * (u + 1))
                    if u > 0:
                        act.wait_ge(ox_ready, u)
                    nc.scalar.activation(o9[:, :, :].rearrange("p c q -> p (c q)"), ps[:, BK_PV, :], ACT.Copy).then_inc(o9_evac, 1)
                if i == 2 and 0 <= s + 2 < UNITS:
                    u = s + 2
                    act.wait_ge(mt_ready, u + 1)
                    if u >= 2:
                        act.wait_ge(max_loaded[u % 2], 16 * (u // 2))
                    nc.scalar.activation(mt[:, u % 2, :], ps[0:48, BK_X, 0:S // 2].bitcast(BF16), ACT.Copy).then_inc(mt_evac, 1)
                if i == 2 and 0 <= s - 2 < UNITS:
                    u = s - 2
                    act.wait_ge(ot_ready, u + 1)
                    if u > 0:
                        act.wait_ge(wo_ready, u)
                    nc.scalar.activation(onT[:, :], ps[:, BK_Y, 0:S], ACT.Identity,
                                         bias=vec[:, VBV + u // B:VBV + u // B + 1]).then_inc(ot_evac, 1)
                if (s, i) in at:
                    evacuate(*at[s, i])
                g = group_of(s, 6)
                if i == 0 and g is not None:
                    act.wait_ge(r1["K"], g + 1)
                    nc.scalar.activation(part["K"][:, 1, :], rest["K"][:, :], ACT.Copy).then_inc(p2["K"], 1)

        @block.vector
        def _(dve):
            v = nc.vector
            v.memset(kst[0][:, :, :, :].rearrange("p n a t -> p (n a t)").bitcast(U32), 0).then_inc(zeroed[0], 1)
            dve.wait_ge(ld_id, 16)
            v.tensor_copy(identb[:, :], ident[:, :]).then_inc(ident_ready, 1)
            def query_mask(g):
                own = slice(GB * g, GB * g + GB)
                dve.wait_ge(ld_mqk[g], 16)
                v.tensor_scalar(mqk[:, own, :], mqk_in[:, own, :], 0.0, NEG, ALU.is_equal, ALU.mult).then_inc(masks_ready, 1)
                dve.wait_ge(masks_ready, g + 1)
                v.tensor_reduce(anyf[:, own], mqk[:, own, :], AX.X, ALU.max).then_inc(mask_step, 1)
                dve.wait_ge(mask_step, g + 1)
                v.tensor_scalar(anyk[:, own], anyf[:, own], 0.0, None, ALU.is_ge).then_inc(flags_ready, 1)

            query_mask(0)

            def key_mask():
                dve.wait_ge(ld_mk, 16)
                v.tensor_scalar(mk[:, :, :], mk_in, 0.0, NEG, ALU.is_equal, ALU.mult).then_inc(bias_rows, 1)
                dve.wait_ge(bias_rows, 1)
                dve.wait_ge(flags_ready, NG)
                v.tensor_reduce(anyf[:, :], mk[:, :, :], AX.X, ALU.max).then_inc(mask_step, 1)
                dve.wait_ge(mask_step, NG + 1)
                v.tensor_scalar(cscale[:, :], anyf[:, :], 0.0, SCALE, ALU.is_ge, ALU.mult).then_inc(mask_step, 1)

            def normalize(n, sums, stats, group):
                dve.wait_ge(rstd_done, n + 1)
                for b in range(GB):
                    last = v.tensor_scalar(norm[:, GB * group + b, :], sums[:, b, :], stats[:, b, 0:1],
                                           rstd[:, n % 2, b:b + 1], ALU.subtract, ALU.mult)
                last.then_inc(norm_done, 1)

            def first_part(m, g):
                if m == "K":
                    dve.wait_ge(g_evac, index["K", g] + 1)
                else:
                    dve.wait_ge(g_evac, index["Q", g] + 1)
                if g > 0:
                    dve.wait_ge((k_stacked if m == "K" else q_stacked)[(g - 1) % STACKS], (k_dmas if m == "K" else q_dmas)(g - 1))
                v.tensor_copy(part[m][:, 0, :], full[m][:, :]).then_inc(p1[m], 1)

            def second_part(m, g):
                dve.wait_ge(r1[m], g + 1)
                v.tensor_copy(part[m][:, 1, :], rest[m][:, :]).then_inc(p2[m], 1)

            for s, i in steps:
                if 0 <= s + LEAD < UNITS:
                    u = s + LEAD
                    n = CH * u + i
                    dve.wait_ge(s_ready, n + 1)
                    if i == 0 and u >= LEAD:
                        dve.wait_ge(nparts_done, u - LEAD + 1)
                    v.tensor_reduce(negm[:, u % LEAD, 4 * i:4 * i + 4], ps[:, BK_S + n % 2, :].rearrange("p (h k) -> p h k", h=4),
                                    AX.X, ALU.max, negate=True).then_inc(max_done, 1)
                u, un = s - 3, s - 2
                if i == 0 and 0 <= u < UNITS:
                    g, b = u // 4, u % 4
                    dve.wait_ge(wo_ready, u + 1)
                    if b == 0:
                        dve.wait_ge(res_done, res_order.index((u // B, g % NG)) + 1)
                        if g > 1:
                            dve.wait_ge(norm_done, norm_index((g - 2) // NG, (g - 2) % NG) + 1)
                    v.tensor_tensor(rsum[:, g % 2, b, :], ps[:, BK_Y, S:2 * S], res[:, GB * (g % NG) + b, :], ALU.add)\
                        .then_inc(resid_done, 1)
                if i == 0 and 0 <= un < UNITS:
                    view = ps[:, BK_X, :].rearrange("p (h e) -> p h e", e=32)
                    dve.wait_ge(ox_ready, un + 1)
                    v.reciprocal(rec[:, :].unsqueeze(2), view[:, :, DK:DK + 1]).then_inc(rec_done, 1)
                if i == 0 and 0 <= u < UNITS:
                    dve.wait_ge(resid_done, u + 1)
                    v.bn_stats(stat[:, b, :], rsum[:, g % 2, b, :]).then_inc(stat_done, 1)
                if i == 0 and 0 <= un < UNITS:
                    dve.wait_ge(rec_done, un + 1)
                    if un > 0:
                        dve.wait_ge(ot_ready, un)
                    v.tensor_tensor(onorm[:, :].rearrange("p (h d) -> p h d", d=DK), view[:, :, 0:DK],
                                    rec[:, :].unsqueeze(2).to_broadcast([128, H, DK]), ALU.mult).then_inc(onorm_done, 1)
                if i == 0 and 0 <= u < UNITS:
                    dve.wait_ge(stat_done, u + 1)
                    v.bn_aggr(mv[:, g % 2, b, :], stat[:, b, :]).then_inc(mv_done, 1)
                g = attention_end(s)
                if i == 3 and g is not None:
                    layer, gg = g // NG, g % NG
                    if g == 0:
                        dve.wait_ge(masks_ready, NG)
                    if layer > 0:
                        before = ("F" if layer == 2 else layer - 1, gg)
                        dve.wait_ge(gain_done, norm_order.index(before) + 2)
                    normalize(norm_index(layer, gg), rsum[:, g % 2, :, :], mv[:, g % 2, :, :], gg)
                kind, g = at.get((s, i), ("", 0))
                if kind == "Q":
                    layer = g // NG
                    dve.wait_ge(g_ready, index["Q", g] + 1)
                    if g > 0:
                        dve.wait_ge(r1["Q"], g)
                    bank = ps[:, BK_G, :]
                    bias = vec[:, VBQ + layer:VBQ + layer + 1]
                    if g == 0:
                        dve.wait_ge(ld_vec, 16)
                    if layer == 0:
                        dve.wait_ge(g_evac, index["A", g] + 1)
                        i_ = v.scalar_tensor_tensor(full["Q"][:, :], bank, bias, qscale[:, :], ALU.add, ALU.mult)
                    elif layer == 1:
                        if g == NG:
                            dve.wait_ge(mask_step, NG + 2)
                        i_ = v.scalar_tensor_tensor(
                            full["Q"][:, :].rearrange("p (b t) -> p b t", b=GB), bank.rearrange("p (b t) -> p b t", b=GB), bias,
                            cscale[:, GB * (g % NG):GB * (g % NG) + GB].unsqueeze(2).to_broadcast([128, GB, S]), ALU.add, ALU.mult)
                    else:
                        i_ = v.tensor_scalar(full["Q"][:, :], bank, bias, SCALE, ALU.add, ALU.mult)
                    i_.then_inc(g_evac, 1)
                if kind == "F2":
                    gg = g % NG
                    dve.wait_ge(g_ready, index["F2", g] + 1)
                    dve.wait_ge(res_done, res_order.index(("F", gg)) + 1)
                    v.tensor_tensor(rsum[:, 2, :, :].rearrange("p b d -> p (b d)"), ps[:, BK_G, :],
                                    res[:, GB * gg:GB * gg + GB, :].rearrange("p b d -> p (b d)"), ALU.add).then_inc(g_evac, 1)
                g = group_of(s, 8, 2 * NG)
                if g is not None and i == 3:
                    dve.wait_ge(g_evac, index["F2", g] + 1)
                    for b in range(GB):
                        last = v.bn_stats(fstat[:, b, :], rsum[:, 2, b, :])
                    last.then_inc(fstat_done, 1)
                    dve.wait_ge(fstat_done, g - 2 * NG + 1)
                    for b in range(GB):
                        last = v.bn_aggr(fmv[:, b, :], fstat[:, b, :])
                    last.then_inc(fmv_done, 1)
                g = group_of(s, 7, 2 * NG)
                if g is not None and i == 1:
                    dve.wait_ge(gain_done, norm_index(1, g % NG) + 2)
                    dve.wait_ge(fmv_done, g - 2 * NG + 1)
                    normalize(norm_index("F", g % NG), rsum[:, 2, :, :], fmv, g % NG)
                for m, slot, step, do in (("K", 7, 1, first_part), ("Q", 6, 1, first_part), ("Q", 5, 0, second_part)):
                    if i == step and group_of(s, slot) is not None:
                        do(m, group_of(s, slot))
                if i == 3 and s in (-5, 0, 3):
                    query_mask({-5: 1, 0: 2, 3: 3}[s])
                if s == 6 and i == 1:
                    key_mask()

        @block.gpsimd
        def _(pool):
            gp = nc.gpsimd
            def constants(n):
                gp.memset(vst[n][:, :, :, DK:32].rearrange("p b h d -> p (b h) d"), 1.0).then_inc(const_ready, 1)
                gp.memset(qst[n][:, :, :].rearrange("p n t -> p (n t)").bitcast(F32), TWO_ONES).then_inc(q_ones[n], 1)

            def zeros(n):
                gp.memset(kst[n][:, :, :, :].rearrange("p n a t -> p (n a t)").bitcast(U32), 0).then_inc(zeroed[n], 1)

            constants(0)
            gp.memset(mhalf[:, :], -0.5)
            gp.memset(zrow[:, :], 0.0)

            def gain_row(j):
                return row[:, R_G + j, :].unsqueeze(1).to_broadcast([128, GB, D])

            def offset_row(j):
                return row[:, R_B + j, :].unsqueeze(1).to_broadcast([128, GB, D])

            def offsets():
                pool.wait_ge(ld_row, 16)
                for j in range(3):
                    last = gp.tensor_tensor(row[:, R_B + j, :], row[:, R_B + j, :], row[:, R_BO + j, :], ALU.add)
                last.then_inc(gain_done, 1)

            def residual_rows(g):
                pool.wait_ge(ld_res[g], 16)
                own = res[:, GB * g:GB * g + GB, :]
                gp.tensor_tensor(own, own, row[:, R_BOSA, :].unsqueeze(1).to_broadcast([128, GB, D]), ALU.add).then_inc(res_done, 1)

            def deviation(n, stats):
                if n > 1:
                    pool.wait_ge(norm_done, n - 1)
                gp.tensor_scalar(vareps[:, n % 2, :].unsqueeze(2), stats[:, :, 1:2], EPS, None, ALU.add).then_inc(vareps_done, 1)
                pool.wait_ge(vareps_done, n + 1)
                gp.tensor_tensor(rstd[:, n % 2, :], vareps[:, n % 2, :], mhalf[:, :], ALU.pow).then_inc(rstd_done, 1)

            def affine(n, layer, gg, half):
                j = {0: 0, 1: 1, "F": 2, 2: 3}[layer]
                if half == 0:
                    pool.wait_ge(norm_done, n + 1)
                if layer == 2:
                    dst = fin[:, gg % 2, :, :]
                    if gg >= 2 and half == 0:
                        pool.wait_ge(stored[gg % 2], 16 * (gg // 2))
                else:
                    dst = res[:, GB * gg:GB * gg + GB, :]
                if half == 0:
                    gp.tensor_tensor(dst, norm[:, GB * gg:GB * gg + GB, :], gain_row(j), ALU.mult).then_inc(gain_done, 1)
                    return
                pool.wait_ge(gain_done, n + 2)
                gp.tensor_tensor(dst, dst, offset_row(j), ALU.add).then_inc(fin_ready if layer == 2 else res_done, 1)

            for s, i in steps:
                if i == 0 and 0 <= s + 2 < UNITS:
                    u = s + 2
                    heads = negm[:, u % LEAD, :].rearrange("p (n a) -> p a n", a=2)
                    left = nrest[:, u % 2, :].rearrange("p (a n) -> p a n", a=2)
                    pt = [nparts[:, u % 2, n, :].rearrange("p (a n) -> p a n", a=2) for n in range(3)]
                    pool.wait_ge(max_done, CH * (u + 1))
                    if u > 1:
                        pool.wait_ge(mt_ready, u - 1)
                    gp.tensor_copy(pt[0], heads).then_inc(nparts_step, 1)
                    pool.wait_ge(nparts_step, 3 * u + 1)
                    gp.tensor_tensor(left, heads, pt[0], ALU.subtract).then_inc(nparts_step, 1)
                    pool.wait_ge(nparts_step, 3 * u + 2)
                    gp.tensor_copy(pt[1], left).then_inc(nparts_step, 1)
                    pool.wait_ge(nparts_step, 3 * u + 3)
                    gp.tensor_tensor(pt[2], left, pt[1], ALU.subtract).then_inc(nparts_done, 1)
                if i == 0 and attention_end(s) is not None:
                    g = attention_end(s)
                    pool.wait_ge(mv_done, 4 * g + 4)
                    deviation(norm_index(g // NG, g % NG), mv[:, g % 2, :, :])
                if i == 0 and group_of(s, 7, 2 * NG) is not None:
                    g = group_of(s, 7, 2 * NG)
                    pool.wait_ge(fmv_done, g - 2 * NG + 1)
                    deviation(norm_index("F", g % NG), fmv)
                for half in range(2):
                    g = attention_end(s - 1)
                    if i == 1 + half and g is not None:
                        affine(norm_index(g // NG, g % NG), g // NG, g % NG, half)
                    g = group_of(s, 7 - 2 * half, 2 * NG)
                    if i == 2 - half and g is not None:
                        affine(norm_index("F", g % NG), "F", g % NG, half)
                if (s, i) == (0, 1):
                    offsets()
                if i == 2 and 1 <= s < NG + 1:
                    residual_rows(s - 1)
                if (s, i) == (-5, 3):
                    constants(1)
                    zeros(1)
                if (s, i) in ((-1, 3), (0, 3)):
                    (zeros if s else constants)(2)
                for m, slot, step in (("K", 7, 1), ("Q", 6, 1)):
                    if i == step and group_of(s, slot) is not None:
                        g = group_of(s, slot)
                        pool.wait_ge(p1[m], g + 1)
                        if g > 0:
                            pool.wait_ge(p2[m], g)
                            pool.wait_ge(p3[m], g)
                        gp.tensor_tensor(rest[m][:, :], full[m][:, :], part[m][:, 0, :], ALU.subtract).then_inc(r1[m], 1)
                for m, slot, step in (("K", 6, 2), ("Q", 5, 2)):
                    if i == step and group_of(s, slot) is not None:
                        g = group_of(s, slot)
                        pool.wait_ge(p2[m], g + 1)
                        gp.tensor_tensor(part[m][:, 2, :], rest[m][:, :], part[m][:, 1, :], ALU.subtract).then_inc(p3[m], 1)


def kernel(**inputs):
    import ml_dtypes as _ml
    import numpy as _np
    import concourse.bacc as _bacc
    from concourse import mybir as _mybir
    from concourse.bass_utils import run_bass_kernel_spmd as _run

    a = {k: _np.asarray(v) for k, v in inputs.items()}

    def to_rows(wt):
        return wt.reshape(PAIRS, 2, DK, D).transpose(3, 1, 2, 0).reshape(D, D)

    def to_col(bias):
        return bias.reshape(PAIRS, 2, DK).transpose(1, 2, 0).reshape(D, 1)

    att = [("L0_xattn_sa_w", "L0_xattn_sa_b"), ("L0_xattn_ca_w", "L0_xattn_ca_b"), ("L1_xattn_W", "L1_xattn_b")]
    weights = _np.concatenate(
        [m for wn, _ in att for m in (to_rows(a[wn + "q"]), to_rows(a[wn + "k"]), a[wn + "v"].T, a[wn + "o"].T)]
        + [a["L0_xattn_ffn_w1"].T]
        + [a["L0_xattn_ffn_w2"].T.reshape(4, 128, D).transpose(1, 0, 2).reshape(128, FF)], axis=1)
    vectors = _np.concatenate(
        [to_col(a[bn + "q"]) for _, bn in att] + [to_col(a[bn + "k"]) for _, bn in att]
        + [a[bn + "v"].reshape(D, 1) for _, bn in att]
        + [a["L0_xattn_ffn_b1"].reshape(4, 128).T]
        + [a[f"L0_xattn_ln{n}_g"].reshape(D, 1) for n in (1, 2, 3)]
        + [a[f"L0_xattn_ln{n}_b"].reshape(D, 1) for n in (1, 2, 3)], axis=1)
    rows = _np.stack(
        [a["L0_xattn_sa_bo"]] + [a[f"L0_xattn_ln{n}_g"] for n in (1, 2, 3)] + [a["L1_xattn_ln_gamma"]]
        + [a[f"L0_xattn_ln{n}_b"] for n in (1, 2, 3)] + [a["L1_xattn_ln_beta"]]
        + [a["L0_xattn_ca_bo"], a["L0_xattn_ffn_b2"], a["L1_xattn_bo"]])
    k_rows = _np.zeros((6, PAIRS, 2, GT), _ml.bfloat16)
    for n in range(3):
        for h in range(2):
            k_rows[2 * n + h, :, h, :] = 1
    arrays = {
        "x_tok": a["x"], "x_t": a["x"].transpose(2, 0, 1).reshape(D, B * S),
        "ctx_t": a["ctx_1024"].transpose(2, 0, 1).reshape(D, B * S),
        "mask_k": a["mask_Bx1x1xS2_if1"].reshape(B, S), "mask_qk": a["mask_Bx1xSxS2_if1"].reshape(B, S, S),
        "weights": weights, "vectors": vectors, "rows": rows, "k_rows": k_rows,
        "ident": _np.eye(128, dtype=_np.float32),
    }
    arrays = {k: _np.ascontiguousarray(v) for k, v in arrays.items()}
    nc = _bacc.Bacc("TRN2", target_bir_lowering=False, num_devices=1)
    args = [nc.dram_tensor("in_" + k, v.shape, _mybir.dt.from_np(v.dtype), kind="ExternalInput").ap() for k, v in arrays.items()]
    args.append(nc.dram_tensor("out_0", (B, S, D), _mybir.dt.float32, kind="ExternalOutput").ap())
    build(nc, *args)
    r = _run(nc, [{"in_" + k: v for k, v in arrays.items()}], core_ids=[0])
    return r.results[0]["out_0"]
```

```python
import concourse.bass as bass
from concourse import mybir
from contextlib import ExitStack

F32 = mybir.dt.float32
BF16 = mybir.dt.bfloat16
I32 = mybir.dt.int32
U32 = mybir.dt.uint32
ALU = mybir.AluOpType
ACT = mybir.ActivationFunctionType
AX = mybir.AxisListType

B, S, D, H, DK, FF = 16, 128, 128, 16, 8, 512
PAIRS = H // 2
LAYERS = 3
GB = 4
GT = GB * S
NG = B // GB
UNITS, GROUPS = LAYERS * B, LAYERS * NG
CH = H // 4
NPROD = 6
Q_PART = [0, 0, 0, 1, 1, 2]
K_PART = [0, 1, 2, 0, 1, 0]
MASK_ROW = 16 * NPROD
MAX_ROW = MASK_ROW + 1
K_SCORES = MAX_ROW
K_SHIFTED = MAX_ROW + 6
SCALE = float(1.0 / DK ** 0.5)
NEG = -float(2 ** 30)
EPS = 1e-5
STACKS = 3
TWO_ONES = 1.0 + 0x3F80 / 2 ** 23
PROBS = 5
V_PAIR, V_ODD = 288, 144
MAXIMA = 3

WQ, WK, WV, WO, WL = 0, D, 2 * D, 3 * D, 4 * D
W1, W2 = LAYERS * WL, LAYERS * WL + FF
WCOLS = W2 + FF
VBQ, VBK, VBV, VB1, VG, VB = 0, 3, 6, 9, 13, 16
VCOLS = 19
R_BOSA, R_G, R_B, R_BO = 0, 1, 5, 9
ROWS = 12
RING = 3
BK_ST, BK_PV, BK_X, BK_Y = 3, 5, 6, 7


STEP = {"FX": -35, "H0": -33, "H1": -33, "H2": -31, "H3": -30, "F2a": -29, "F2b": -28, "F2 sum": -28,
    "F stats": -27, "F deviation": -27, "F normalize": -25, "F gain": -24, "F offset": -23, "K": -27,
    "K first": -26, "K rest": -26, "K stack 0": -26, "K stack 3": -26, "K stack 5": -26, "K second": -23,
    "K stack 1": -25, "K stack 4": -25, "K third": -24, "K stack 2": -21, "A": -25, "X": -24, "Q": -23,
    "V": -21, "Q sum": -23, "Q first": -22, "Q rest": -21, "Q stack 0": -19, "Q stack 1": -19,
    "Q stack 2": -19, "Q second": -18, "Q stack 3": -18, "Q stack 4": -18, "Q third": -19, "Q stack 5": -18}
EARLY = {("K", 0): -29, ("A", 0): -27, ("Q", 0): -24, ("V", 0): -22, ("K", 1): -36, ("V", 1): -35,
    ("A", 1): -33, ("Q", 1): -29, ("Q sum", 1): -32}
UNIT_STEP = {"max parts": -9, "max transpose": -6, "max evacuation": -6, "max stack": -5, "o evacuation": 5,
    "o transpose": 7, "o normalize": 8, "on transpose": 10, "on evacuation": 10, "wo": 11, "residual": 12,
    "scores": -12}
VALUES = 2
NORM_STEP = {"deviation": 24, "normalize": 27, "gain": 27, "offset": 32, "store": 33}
ONCE = {"max rows 1": -15, "max rows 2": 3, "mask load 2": -7, "mask load 3": 0, "mask 1": -21, "mask 2": 2,
    "mask 3": 13, "row load": -5, "residual load 0": 1, "residual load 1": 5, "residual load 2": 11,
    "residual load 3": 13, "key mask load": 17, "weight load": 21, "context load 0": 25, "context load 1": 29,
    "context load 2": 34, "context load 3": 37, "key mask": 21, "offsets": 2, "residual rows 0": 10,
    "residual rows 1": 11, "residual rows 2": 14, "residual rows 3": 21, "constants 1": -16, "zeros 1": -15,
    "constants 2": -2, "zeros 2": 3}
FEED_FORWARD = ("FX", "H0", "H1", "H2", "H3", "F2a", "F2b", "F2 sum", "F stats", "F deviation", "F normalize", "F gain", "F offset")


def group_at(s, i, stage):
    for (name, g), step in EARLY.items():
        if name == stage and 4 * s + i == 16 * g + step:
            return g
    g, off = divmod(4 * s + i - STEP[stage], 16)
    first, end = 0, GROUPS
    if stage in FEED_FORWARD:
        first = 2 * NG
    elif stage == "X":
        first = NG
    elif stage == "A":
        end = NG
    return g if off == 0 and first <= g < end and (stage, g) not in EARLY else None


def unit_at(s, i, stage):
    u, off = divmod(4 * s + i - UNIT_STEP[stage], 4)
    return u if off == 0 and 0 <= u < UNITS else None


def norm_at(s, i, stage):
    g, off = divmod(4 * s + i - NORM_STEP[stage], 16)
    return g if off == 0 and 0 <= g < GROUPS else None


def once(s, i, stage):
    return 4 * s + i == ONCE[stage]


def done_before(stage, u, other, tie):
    count = (4 * u + UNIT_STEP[stage] - UNIT_STEP[other] - (0 if tie else 1)) // 4 + 1
    return max(0, min(count, UNITS))


def tasks_at(s, i):
    found = [(stage, group_at(s, i, stage)) for stage in ("K", "A", "X", "Q", "V", "FX", "H0", "H1", "H2", "H3", "F2a", "F2b")]
    return [(stage, g) for stage, g in found if g is not None]


def build(nc, x_tok, x_t, ctx_t, mask_k, mask_qk, weights, vectors, rows, k_rows, ident_in, out):
    first_slot, last_slot = -8, UNITS + 4
    steps = [(s, i) for s in range(first_slot, last_slot + 1) for i in range(CH)]
    tasks = [task for s, i in steps for task in tasks_at(s, i)]
    index = {task: n for n, task in enumerate(t for t in tasks if t[0] != "F2a")}

    users = []
    for s, i in steps:
        n = CH * s + i - UNIT_STEP["scores"]
        if 0 <= n < CH * UNITS:
            users.append(("S", n))
        users += [task for task in tasks_at(s, i) if task[0] != "F2b"]
    turn = {user: n for n, user in enumerate(users)}
    act_order = [task for task in tasks if task[0] not in ("Q", "F2a", "F2b")]
    dve_order = []
    for s, i in steps:
        for kind, stage in (("Q", "Q sum"), ("F2a", "F2 sum")):
            if group_at(s, i, stage) is not None:
                dve_order.append((kind, group_at(s, i, stage)))

    ctx = ExitStack()
    with ctx:
        def sb(name, shape, dt=F32):
            return ctx.enter_context(nc.sbuf_tensor(name, shape, dt))

        def sem(name):
            return ctx.enter_context(nc.semaphore(name))

        w = sb("w", [128, WCOLS])
        vec = sb("vec", [128, VCOLS])
        row = sb("row", [128, ROWS, D])
        ident = sb("ident", [128, 128])
        identb = sb("identb", [128, 128], BF16)
        xt = sb("xt", [128, B * S])
        ct = sb("ct", [128, B * S])
        res = sb("res", [128, B, D])
        norm = sb("norm", [128, B, D])
        rsum = sb("rsum", [128, 3, GB, D])
        stat = sb("stat", [128, GB, 6])
        mv = sb("mv", [128, 2, GB, 2])
        fstat = sb("fstat", [128, GB, 6])
        fmv = sb("fmv", [128, GB, 2])
        rstd = sb("rstd", [128, 2, GB])
        vareps = sb("vareps", [128, 2, GB])
        mhalf = sb("mhalf", [128, GB])
        xg = sb("xg", [128, GT])
        hid = sb("hid", [128, 4, GT])
        qst = [sb(f"qst{n}", [128, PAIRS, GT], BF16) for n in range(STACKS)]
        kst = [sb(f"kst{n}", [128, PAIRS, 2, GT], BF16) for n in range(STACKS)]
        vst = [sb(f"vst{n}", [128, GB * CH // 2, V_PAIR]) for n in range(STACKS)]
        full = {m: sb(f"full{m}", [128, GT]) for m in "QK"}
        rest = {m: sb(f"rest{m}", [128, GT]) for m in "QK"}
        part = {m: sb(f"part{m}", [128, 3, GT], BF16) for m in "QK"}
        probs = sb("probs", [128, PROBS, 4, S])
        qscale = sb("qscale", [128, GT])
        cscale = sb("cscale", [128, B])
        anyk = sb("anyk", [128, B], BF16)
        anyf = sb("anyf", [128, B])
        mqk = sb("mqk", [128, B, S], BF16)
        mk = sb("mk", [128, B, S], BF16)
        zrow = sb("zrow", [1, GT], BF16)
        negm = sb("negm", [128, MAXIMA, H])
        nrest = sb("nrest", [128, 2, H])
        nparts = sb("nparts", [128, 2, 3, H], BF16)
        mt = sb("mt", [48, 2, S], BF16)
        o9 = sb("o9", [128, CH // 2, S])
        rec = sb("rec", [128, H])
        onorm = sb("onorm", [128, D])
        onT = sb("onT", [128, S])
        fin = sb("fin", [128, 2, GB, D])
        ps = ctx.enter_context(nc.psum_tensor("ps", [128, 8, 512], F32))
        mqk_in = norm[:, :, :].bitcast(I32)
        mk_in = hid[:, :, :].bitcast(I32).rearrange("p a (b k) -> p (a b) k", k=S)

        ld_w, ld_w2, ld_x2, ld_vec, ld_row, ld_id = sem("ld_w"), sem("ld_w2"), sem("ld_x2"), sem("ld_vec"), sem("ld_row"), sem("ld_id")
        ld_x, ld_c, ld_res, ld_mk = sem("ld_x"), [sem(f"ld_c{g}") for g in range(NG)], [sem(f"ld_res{g}") for g in range(NG)], sem("ld_mk")
        ld_mqk = [sem(f"ld_mqk{g}") for g in range(NG)]
        zeroed = [sem(f"zeroed{n}") for n in range(STACKS)]
        q_ones = [sem(f"q_ones{n}") for n in range(STACKS)]
        ld_rows = [sem(f"ld_rows{n}") for n in range(STACKS)]
        k_stacked = [sem(f"k_stacked{n}") for n in range(STACKS)]
        q_stacked = [sem(f"q_stacked{n}") for n in range(STACKS)]
        ident_ready, const_ready, masks_ready = sem("ident_ready"), sem("const_ready"), sem("masks_ready")
        mask_step, flags_ready, bias_rows = sem("mask_step"), sem("flags_ready"), sem("bias_rows")
        g_ready = sem("g_ready")
        act_evac, dve_evac = sem("act_evac"), sem("dve_evac")
        s_ready, max_done = sem("s_ready"), sem("max_done")
        nparts_step, nparts_done, mt_ready, mt_evac = sem("nparts_step"), sem("nparts_done"), sem("mt_ready"), sem("mt_evac")
        max_loaded = [sem("max_loaded0"), sem("max_loaded1")]
        st_ready, exp_done, pv_done, o9_evac = sem("st_ready"), sem("exp_done"), sem("pv_done"), sem("o9_evac")
        ox_ready, rec_done, onorm_done, ot_ready, ot_evac = (
            sem("ox_ready"), sem("rec_done"), sem("onorm_done"), sem("ot_ready"), sem("ot_evac"))
        wo_ready, resid_done, stat_done, mv_done = sem("wo_ready"), sem("resid_done"), sem("stat_done"), sem("mv_done")
        fres_done, fstat_done, fmv_done = sem("fres_done"), sem("fstat_done"), sem("fmv_done")
        vareps_done, rstd_done, norm_done, gain_done, res_done = (
            sem("vareps_done"), sem("rstd_done"), sem("norm_done"), sem("gain_done"), sem("res_done"))
        p1 = {m: sem(f"part1_{m}") for m in "QK"}
        r1 = {m: sem(f"rest_{m}") for m in "QK"}
        p2 = {m: sem(f"part2_{m}") for m in "QK"}
        p3 = {m: sem(f"part3_{m}") for m in "QK"}
        gained = sem("gained")
        blank = sem("blank")
        fin_ready, stored = sem("fin_ready"), [sem("stored0"), sem("stored1")]

        def ring(*user):
            return ps[:, turn[user] % RING, :]

        def evacuated(kind, g):
            if kind in ("Q", "F2a"):
                return dve_evac, dve_order.index((kind, g)) + 1
            return act_evac, act_order.index((kind, g)) + 1

        def bank_read(*user):
            if turn[user] < RING:
                return None
            kind, n = users[turn[user] - RING]
            return (max_done, n + 1) if kind == "S" else evacuated(kind, n)

        def mask_dma(g):
            return NG <= g < 2 * NG or 2 * NG <= g < 2 * NG + STACKS

        def k_dmas(g):
            return 16 * sum(2 * NPROD + (1 if mask_dma(o) else 0) for o in range(g % STACKS, g + 1, STACKS))

        def q_dmas(g):
            return 16 * NPROD * (g // STACKS + 1)

        def norm_index(layer, g):
            return norm_order.index((layer, g))

        norm_order = []
        for s, i in steps:
            g = norm_at(s, i, "normalize")
            if g is not None:
                norm_order.append((g // NG, g % NG))
            g = group_at(s, i, "F normalize")
            if g is not None:
                norm_order.append(("F", g % NG))
        res_order = [(0, g) for g in range(NG)]
        for layer, g in norm_order:
            if layer != 2:
                res_order.append(({0: 1, 1: "F", "F": 2}[layer], g))
        source = {1: 0, 2: "F"}

        block = ctx.enter_context(nc.Block())

        @block.sync
        def _(sp):
            sp.dma_start(w[:, 0:WL], weights[:, 0:WL]).then_inc(ld_w, 16)
            sp.dma_start(xt[:, 0:GT], x_t[:, 0:GT]).then_inc(ld_x, 16)
            sp.dma_start(vec[:, :], vectors).then_inc(ld_vec, 16)
            sp.dma_start(ident[:, :], ident_in).then_inc(ld_id, 16)

            def query_mask(g):
                sp.dma_start(mqk_in[:, GB * g:GB * g + GB, :], mask_qk[GB * g:GB * g + GB].rearrange("b q k -> q b k"))\
                    .then_inc(ld_mqk[g], 16)

            def max_rows(n):
                sp.wait_ge(zeroed[n], 1)
                sp.dma_start(kst[n][MAX_ROW:K_SHIFTED, :, :, :], k_rows).then_inc(ld_rows[n], 16)

            query_mask(0)
            max_rows(0)
            sp.dma_start(xt[:, GT:B * S], x_t[:, GT:B * S]).then_inc(ld_x2, 16)
            query_mask(1)

            def row_load(_):
                sp.dma_start(row[:, :, :], rows.partition_broadcast(128)).then_inc(ld_row, 16)

            def residual_load(g):
                sp.dma_start(res[:, GB * g:GB * g + GB, :], x_tok[GB * g:GB * g + GB].rearrange("b t d -> t b d")).then_inc(ld_res[g], 16)

            def context_load(g):
                sp.dma_start(ct[:, GT * g:GT * g + GT], ctx_t[:, GT * g:GT * g + GT]).then_inc(ld_c[g], 16)

            def key_mask_load(_):
                sp.dma_start(mk_in, mask_k.partition_broadcast(128)).then_inc(ld_mk, 16)

            def weight_load(_):
                sp.dma_start(w[:, WL:WCOLS], weights[:, WL:WCOLS]).then_inc(ld_w2, 16)

            later = [("max rows 1", max_rows, 1), ("mask load 2", query_mask, 2), ("row load", row_load, None),
                     ("mask load 3", query_mask, 3), ("max rows 2", max_rows, 2), ("key mask load", key_mask_load, None),
                     ("weight load", weight_load, None)]
            later += [(f"residual load {n}", residual_load, n) for n in range(NG)]
            later += [(f"context load {n}", context_load, n) for n in range(NG)]

            def stack_free(g):
                if g >= STACKS:
                    sp.wait_ge(st_ready, 4 * CH * (g - STACKS + 1))
                else:
                    sp.wait_ge(ld_rows[g], 16)

            first_k, first_q = (min(range(NPROD), key=lambda c: STEP[f"{m} stack {c}"]) for m in "KQ")
            assert STEP[f"K stack {first_k}"] < STEP[f"Q stack {first_q}"]

            def stack_k(g, c):
                for a in range(2):
                    sp.dma_start(kst[g % STACKS][16 * c + 8 * a:16 * c + 8 * a + 8, :, a, :],
                                 part["K"][64 * a:64 * a + 64, K_PART[c], :]).then_inc(k_stacked[g % STACKS], 16)

            def stack_q(g, c):
                sp.dma_start(qst[g % STACKS][16 * c:16 * c + 16, :, :],
                             part["Q"][:, Q_PART[c], :]).then_inc(q_stacked[g % STACKS], 16)

            for s, i in steps:
                u = unit_at(s, i, "max stack")
                if u is not None:
                    g, b = u // 4, u % 4
                    sp.wait_ge(mt_evac, u + 1)
                    sp.dma_start(qst[g % STACKS][MAX_ROW:MAX_ROW + 6, :, b * S:(b + 1) * S],
                                 mt[:, u % 2, :]).then_inc(max_loaded[u % 2], 16)
                for c in range(NPROD):
                    g = group_at(s, i, f"K stack {c}")
                    if g is not None:
                        if c == first_k:
                            stack_free(g)
                        sp.wait_ge((p1["K"], p2["K"], p3["K"])[K_PART[c]], g + 1)
                        stack_k(g, c)
                        if c == 0 and mask_dma(g):
                            src = zrow[0:1, :]
                            if g < 2 * NG:
                                sp.wait_ge(bias_rows, 1)
                                src = mk[0:1, :, :].rearrange("p b k -> p (b k)")[:, (g % NG) * GT:(g % NG + 1) * GT]
                            sp.dma_start(kst[g % STACKS][MASK_ROW:MASK_ROW + 1, :, :, :].rearrange("o p a t -> o (p a) t"),
                                         src.unsqueeze(1).to_broadcast([1, 2 * PAIRS, GT])).then_inc(k_stacked[g % STACKS], 16)
                for c in range(NPROD):
                    g = group_at(s, i, f"Q stack {c}")
                    if g is not None:
                        if c == first_q and g < STACKS:
                            sp.wait_ge(q_ones[g], 1)
                        sp.wait_ge((p1["Q"], p2["Q"], p3["Q"])[Q_PART[c]], g + 1)
                        stack_q(g, c)
                for name, load, n in later:
                    if once(s, i, name):
                        load(n)
                g = norm_at(s, i, "store")
                if g is not None and g >= 2 * NG:
                    g -= 2 * NG
                    sp.wait_ge(fin_ready, g + 1)
                    sp.dma_start(out[GB * g:GB * g + GB].rearrange("b t d -> t b d"),
                                 fin[:, g % 2, :, :]).then_inc(stored[g % 2], 16)
            sp.wait_ge(stored[0], 16 * (NG // 2))
            sp.wait_ge(stored[1], 16 * (NG // 2))

        @block.tensor
        def _(pe):
            mm = nc.tensor.matmul

            def scores(u, i):
                g, b, n = u // 4, u % 4, CH * u + i
                q, k, tok = qst[g % STACKS], kst[g % STACKS], slice(b * S, (b + 1) * S)
                if b == 0 and i == 0:
                    pe.wait_ge(k_stacked[g % STACKS], k_dmas(g))
                    pe.wait_ge(q_stacked[g % STACKS], q_dmas(g))
                    if g < STACKS:
                        pe.wait_ge(ld_rows[g], 16)
                if bank_read("S", n):
                    pe.wait_ge(*bank_read("S", n))
                bank = ring("S", n)
                masked = u < B
                if masked:
                    if b == 0 and i == 0:
                        pe.wait_ge(masks_ready, g + 1)
                    mm(bank.rearrange("p (h k) -> p h k", h=4), identb[:, :],
                       mqk[:, u, :].unsqueeze(1).to_broadcast([128, 4, S]), start=True, stop=False, skip_group_check=True)
                for j in range(2):
                    p = 2 * i + j
                    last = mm(bank[:, 256 * j:256 * j + 256].rearrange("p (a k) -> p a k", a=2), q[0:K_SCORES, p, tok],
                              k[0:K_SCORES, p, :, tok], start=not masked, stop=True, skip_group_check=True)
                last.then_inc(s_ready, 1)

            def shifted_scores(u, i):
                g, b, n = u // 4, u % 4, CH * u + i
                q, k, tok = qst[g % STACKS], kst[g % STACKS], slice(b * S, (b + 1) * S)
                if i == 0:
                    pe.wait_ge(max_loaded[u % 2], 16 * (u // 2 + 1))
                if n >= 2:
                    pe.wait_ge(exp_done, n - 1)
                bank = ps[:, BK_ST + n % 2, :]
                masked = u < B
                if masked:
                    mm(bank.rearrange("p (h q) -> p h q", h=4), mqk[:, u, :],
                       identb[:, :].unsqueeze(1).to_broadcast([128, 4, S]), start=True, stop=False, skip_group_check=True)
                for c in range(4):
                    p, a = 2 * i + c // 2, c % 2
                    last = mm(bank[:, c * S:(c + 1) * S], k[0:K_SHIFTED, p, a, tok], q[0:K_SHIFTED, p, tok],
                              start=not masked, stop=True, skip_group_check=True)
                last.then_inc(st_ready, 1)

            def values(n):
                u, i = n // CH, n % CH
                g, b = u // 4, u % 4
                pe.wait_ge(exp_done, n + 1)
                if i == 0:
                    if b == 0:
                        pe.wait_ge(*evacuated("V", g))
                    if u > 0:
                        pe.wait_ge(o9_evac, u)
                    else:
                        pe.wait_ge(const_ready, 1)
                odd = i % 2
                for c in range(4):
                    last = mm(ps[32 * c:32 * c + 32, BK_PV, (i // 2) * S:(i // 2 + 1) * S],
                              vst[g % STACKS][:, 2 * b + i // 2, 128 * odd + 32 * c:128 * odd + 32 * c + 32],
                              probs[:, n % PROBS, c, :], start=not odd, stop=bool(odd), tile_position=(0, 32 * c),
                              skip_group_check=True)
                last.then_inc(pv_done, 1)

            def transposed_rows(bank, source_rows, g, n):
                pe.wait_ge(norm_done, n + 1)
                for b in range(GB):
                    last = nc.tensor.transpose(bank[:, b * S:(b + 1) * S], source_rows[:, GB * (g % NG) + b, :], ident[:, :])
                return last

            def group_task(kind, g):
                layer, gg = g // NG, g % NG
                if kind != "F2b" and bank_read(kind, g):
                    pe.wait_ge(*bank_read(kind, g))
                bank = ring("F2a" if kind == "F2b" else kind, g)
                ctxs = xt if layer == 0 else ct
                tok = slice(gg * GT, (gg + 1) * GT)
                if kind == "K" and g == 1:
                    pe.wait_ge(ld_x2, 16)
                if kind == "K" and NG <= g < 2 * NG:
                    pe.wait_ge(ld_c[gg], 16)
                if kind == "K" and g == NG:
                    pe.wait_ge(ld_w2, 16)
                if kind == "A":
                    pe.wait_ge(flags_ready, gg + 1)
                    pe.wait_ge(ident_ready, 1)
                    for b in range(GB):
                        last = mm(bank[:, b * S:(b + 1) * S], anyk[:, GB * gg + b:GB * gg + b + 1].to_broadcast([128, 128]),
                                  identb[:, :], start=True, stop=True)
                elif kind == "K":
                    if g == 0:
                        pe.wait_ge(ld_w, 16)
                        pe.wait_ge(ld_x, 16)
                    last = mm(bank, w[:, layer * WL + WK:layer * WL + WK + D], ctxs[:, tok], start=True, stop=True)
                elif kind == "V":
                    for b in range(GB):
                        last = mm(bank[:, b * D:(b + 1) * D], ctxs[:, (GB * gg + b) * S:(GB * gg + b + 1) * S],
                                  w[:, layer * WL + WV:layer * WL + WV + D], start=True, stop=True)
                elif kind == "Q":
                    if layer > 0:
                        pe.wait_ge(*evacuated("X", g))
                    src = xt[:, tok] if layer == 0 else xg[:, :]
                    last = mm(bank, w[:, layer * WL + WQ:layer * WL + WQ + D], src, start=True, stop=True)
                elif kind == "X":
                    last = transposed_rows(bank, norm, g, norm_index(source[layer], gg))
                elif kind == "FX":
                    last = transposed_rows(bank, norm, g, norm_index(1, gg))
                elif kind[0] == "H":
                    j = int(kind[1])
                    pe.wait_ge(*evacuated("FX", g))
                    last = mm(bank, w[:, W1 + j * 128:W1 + (j + 1) * 128], xg[:, :], start=True, stop=True)
                else:
                    pe.wait_ge(*evacuated("H3", g))
                    for b in (range(GB // 2) if kind == "F2a" else range(GB // 2, GB)):
                        for j in range(4):
                            last = mm(bank[:, b * D:(b + 1) * D], hid[:, j, b * S:(b + 1) * S],
                                      w[:, W2 + j * D:W2 + (j + 1) * D], start=j == 0, stop=j == 3)
                if kind != "F2a":
                    last.then_inc(g_ready, 1)

            for s, i in steps:
                n = CH * s + i - UNIT_STEP["scores"]
                if 0 <= n < CH * UNITS:
                    scores(n // CH, n % CH)
                if 0 <= s < UNITS:
                    shifted_scores(s, i)
                u = unit_at(s, i, "max transpose")
                if u is not None:
                    pe.wait_ge(nparts_done, u + 1)
                    if u > 0:
                        pe.wait_ge(mt_evac, u)
                    if done_before("max transpose", u, "o transpose", False) > 0:
                        pe.wait_ge(onorm_done, done_before("max transpose", u, "o transpose", False))
                    if u == 0:
                        pe.wait_ge(ident_ready, 1)
                    nc.tensor.transpose(ps[0:48, BK_X, 0:S // 2].bitcast(BF16), nparts[:, u % 2, :, :].rearrange("p n h -> p (n h)"),
                                        identb[:, :]).then_inc(mt_ready, 1)
                u = unit_at(s, i, "on transpose")
                if u is not None:
                    pe.wait_ge(onorm_done, u + 1)
                    if u > 0:
                        pe.wait_ge(resid_done, u)
                    nc.tensor.transpose(ps[:, BK_Y, 0:S], onorm[:, :], ident[:, :]).then_inc(ot_ready, 1)
                n = CH * s + i - VALUES
                if 0 <= n < CH * UNITS:
                    values(n)
                u = unit_at(s, i, "o transpose")
                if u is not None:
                    pe.wait_ge(o9_evac, u + 1)
                    if u > 0:
                        pe.wait_ge(onorm_done, u)
                    pe.wait_ge(mt_evac, done_before("o transpose", u, "max transpose", True))
                    if u == 0:
                        pe.wait_ge(ld_id, 16)
                    for j in range(CH // 2):
                        last = nc.tensor.transpose(ps[:, BK_X, j * S:(j + 1) * S], o9[:, j, :], ident[:, :])
                    last.then_inc(ox_ready, 1)
                u = unit_at(s, i, "wo")
                if u is not None:
                    layer = u // B
                    pe.wait_ge(ot_evac, u + 1)
                    mm(ps[:, BK_Y, S:2 * S], onT[:, :], w[:, layer * WL + WO:layer * WL + WO + D],
                       start=True, stop=True).then_inc(wo_ready, 1)
                for kind, g in tasks_at(s, i):
                    group_task(kind, g)

        @block.scalar
        def _(act):
            def evacuate(kind, g):
                layer, gg = g // NG, g % NG
                if kind in ("Q", "F2a", "F2b"):
                    return
                bank = ring(kind, g)
                act.wait_ge(g_ready, index[kind, g] + 1)
                if kind == "A":
                    if g > 0:
                        act.wait_ge(*evacuated("Q", g - 1))
                    i_ = nc.scalar.activation(qscale[:, :], bank, ACT.Copy, scale=SCALE)
                elif kind == "K":
                    if g == 0:
                        act.wait_ge(ld_vec, 16)
                    else:
                        act.wait_ge(r1["K"], g)
                    i_ = nc.scalar.activation(full["K"][:, :], bank, ACT.Identity, bias=vec[:, VBK + layer:VBK + layer + 1])
                elif kind == "V":
                    if g >= STACKS:
                        act.wait_ge(pv_done, 4 * CH * (g - STACKS + 1))
                    if g < STACKS:
                        act.wait_ge(const_ready, g + 1)
                    own = vst[g % STACKS][:, :, :].rearrange("p n (o e) -> p (n o) e", e=V_ODD)[:, :, 0:4 * 32]
                    i_ = nc.scalar.activation(own.rearrange("p n (c e) -> p n c e", e=32)[:, :, :, 0:DK],
                                              bank.rearrange("p (n c d) -> p n c d", c=4, d=DK), ACT.Copy)
                elif kind in ("X", "FX"):
                    m = 1 if kind == "FX" else (0 if layer == 1 else 2)
                    i_ = nc.scalar.activation(xg[:, :], bank, ACT.Identity, scale=vec[:, VG + m:VG + m + 1],
                                              bias=vec[:, VB + m:VB + m + 1])
                else:
                    j = int(kind[1])
                    i_ = nc.scalar.activation(hid[:, j, :], bank, ACT.Relu, bias=vec[:, VB1 + j:VB1 + j + 1])
                i_.then_inc(act_evac, 1)

            for s, i in steps:
                if 0 <= s < UNITS:
                    n = CH * s + i
                    act.wait_ge(st_ready, n + 1)
                    if n >= PROBS:
                        act.wait_ge(pv_done, n - PROBS + 1)
                    nc.scalar.activation(probs[:, n % PROBS, :, :].rearrange("p h q -> p (h q)"),
                                         ps[:, BK_ST + n % 2, :], ACT.Exp).then_inc(exp_done, 1)
                u = unit_at(s, i, "o evacuation")
                if u is not None:
                    act.wait_ge(pv_done, CH * (u + 1))
                    if u > 0:
                        act.wait_ge(ox_ready, u)
                    nc.scalar.activation(o9[:, :, :].rearrange("p c q -> p (c q)"), ps[:, BK_PV, 0:CH // 2 * S], ACT.Copy).then_inc(o9_evac, 1)
                u = unit_at(s, i, "max evacuation")
                if u is not None:
                    act.wait_ge(mt_ready, u + 1)
                    if u >= 2:
                        act.wait_ge(max_loaded[u % 2], 16 * (u // 2))
                    nc.scalar.activation(mt[:, u % 2, :], ps[0:48, BK_X, 0:S // 2].bitcast(BF16), ACT.Copy).then_inc(mt_evac, 1)
                u = unit_at(s, i, "on evacuation")
                if u is not None:
                    act.wait_ge(ot_ready, u + 1)
                    if u > 0:
                        act.wait_ge(wo_ready, u)
                    nc.scalar.activation(onT[:, :], ps[:, BK_Y, 0:S], ACT.Identity,
                                         bias=vec[:, VBV + u // B:VBV + u // B + 1]).then_inc(ot_evac, 1)
                for kind, g in tasks_at(s, i):
                    evacuate(kind, g)
                g = group_at(s, i, "K second")
                if g is not None:
                    act.wait_ge(r1["K"], g + 1)
                    nc.scalar.activation(part["K"][:, 1, :], rest["K"][:, :], ACT.Copy).then_inc(p2["K"], 1)

        @block.vector
        def _(dve):
            v = nc.vector
            v.memset(kst[0][:, :, :, :].rearrange("p n a t -> p (n a t)").bitcast(U32), 0).then_inc(zeroed[0], 1)
            dve.wait_ge(ld_id, 16)
            v.tensor_copy(identb[:, :], ident[:, :]).then_inc(ident_ready, 1)
            def query_mask(g):
                own = slice(GB * g, GB * g + GB)
                dve.wait_ge(ld_mqk[g], 16)
                v.tensor_scalar(mqk[:, own, :], mqk_in[:, own, :], 0.0, NEG, ALU.is_equal, ALU.mult).then_inc(masks_ready, 1)
                dve.wait_ge(masks_ready, g + 1)
                v.tensor_reduce(anyf[:, own], mqk[:, own, :], AX.X, ALU.max).then_inc(mask_step, 1)
                dve.wait_ge(mask_step, g + 1)
                v.tensor_scalar(anyk[:, own], anyf[:, own], 0.0, None, ALU.is_ge).then_inc(flags_ready, 1)

            query_mask(0)

            def key_mask():
                dve.wait_ge(ld_mk, 16)
                v.tensor_scalar(mk[:, :, :], mk_in, 0.0, NEG, ALU.is_equal, ALU.mult).then_inc(bias_rows, 1)
                dve.wait_ge(bias_rows, 1)
                dve.wait_ge(flags_ready, NG)
                v.tensor_reduce(anyf[:, :], mk[:, :, :], AX.X, ALU.max).then_inc(mask_step, 1)
                dve.wait_ge(mask_step, NG + 1)
                v.tensor_scalar(cscale[:, :], anyf[:, :], 0.0, SCALE, ALU.is_ge, ALU.mult).then_inc(mask_step, 1)

            def normalize(n, sums, stats, group):
                dve.wait_ge(rstd_done, n + 1)
                for b in range(GB):
                    last = v.tensor_scalar(norm[:, GB * group + b, :], sums[:, b, :], stats[:, b, 0:1],
                                           rstd[:, n % 2, b:b + 1], ALU.subtract, ALU.mult)
                last.then_inc(norm_done, 1)

            def last_rows(n, sums, stats, group):
                dve.wait_ge(ld_row, 16)
                dve.wait_ge(mv_done, UNITS)
                for b in range(GB):
                    last = v.scalar_tensor_tensor(norm[:, GB * group + b, :], sums[:, b, :], stats[:, b, 0:1],
                                                  row[:, R_G + 3, :], ALU.subtract, ALU.mult)
                last.then_inc(gained, 1)
                dve.wait_ge(gained, 1)
                dve.wait_ge(rstd_done, n + 1)
                dve.wait_ge(stored[group % 2], 16 * (group // 2))
                for b in range(GB):
                    last = v.scalar_tensor_tensor(fin[:, group % 2, b, :], norm[:, GB * group + b, :], rstd[:, n % 2, b:b + 1],
                                                  row[:, R_B + 3, :], ALU.mult, ALU.add)
                last.then_inc(fin_ready, 1)

            def first_part(m, g):
                if m == "K":
                    dve.wait_ge(*evacuated("K", g))
                else:
                    dve.wait_ge(*evacuated("Q", g))
                if g > 0:
                    dve.wait_ge((k_stacked if m == "K" else q_stacked)[(g - 1) % STACKS], (k_dmas if m == "K" else q_dmas)(g - 1))
                v.tensor_copy(part[m][:, 0, :], full[m][:, :]).then_inc(p1[m], 1)

            def second_part(m, g):
                dve.wait_ge(r1[m], g + 1)
                v.tensor_copy(part[m][:, 1, :], rest[m][:, :]).then_inc(p2[m], 1)

            for s, i in steps:
                n = CH * s + i - UNIT_STEP["scores"]
                if 0 <= n < CH * UNITS:
                    u, c = n // CH, n % CH
                    dve.wait_ge(s_ready, n + 1)
                    if c == 0 and u >= MAXIMA:
                        dve.wait_ge(nparts_done, u - MAXIMA + 1)
                    v.tensor_reduce(negm[:, u % MAXIMA, 4 * c:4 * c + 4], ring("S", n).rearrange("p (h k) -> p h k", h=4),
                                    AX.X, ALU.max, negate=True).then_inc(max_done, 1)
                u, un = unit_at(s, i, "residual"), unit_at(s, i, "o normalize")
                if u is not None:
                    g, b = u // 4, u % 4
                    dve.wait_ge(wo_ready, u + 1)
                    if b == 0:
                        dve.wait_ge(res_done, res_order.index((u // B, g % NG)) + 1)
                        if g > 1:
                            dve.wait_ge(norm_done, norm_index((g - 2) // NG, (g - 2) % NG) + 1)
                    v.tensor_tensor(rsum[:, g % 2, b, :], ps[:, BK_Y, S:2 * S], res[:, GB * (g % NG) + b, :], ALU.add)\
                        .then_inc(resid_done, 1)
                if un is not None:
                    view = ps[:, BK_X, 0:2 * S].rearrange("p (h e) -> p h e", e=16)
                    dve.wait_ge(ox_ready, un + 1)
                    v.reciprocal(rec[:, :].unsqueeze(2), view[:, :, DK:DK + 1]).then_inc(rec_done, 1)
                if u is not None:
                    dve.wait_ge(resid_done, u + 1)
                    v.bn_stats(stat[:, b, :], rsum[:, g % 2, b, :]).then_inc(stat_done, 1)
                if un is not None:
                    dve.wait_ge(rec_done, un + 1)
                    if un > 0:
                        dve.wait_ge(ot_ready, un)
                    v.tensor_tensor(onorm[:, :].rearrange("p (h d) -> p h d", d=DK), view[:, :, 0:DK],
                                    rec[:, :].unsqueeze(2).to_broadcast([128, H, DK]), ALU.mult).then_inc(onorm_done, 1)
                if u is not None:
                    dve.wait_ge(stat_done, u + 1)
                    v.bn_aggr(mv[:, g % 2, b, :], stat[:, b, :]).then_inc(mv_done, 1)
                g = norm_at(s, i, "normalize")
                if g is not None:
                    layer, gg = g // NG, g % NG
                    if g == 0:
                        dve.wait_ge(masks_ready, NG)
                    if layer > 0:
                        before = ("F" if layer == 2 else layer - 1, gg)
                        dve.wait_ge(gain_done, norm_order.index(before) + 2)
                    if g < GROUPS - 1:
                        normalize(norm_index(layer, gg), rsum[:, g % 2, :, :], mv[:, g % 2, :, :], gg)
                    else:
                        last_rows(norm_index(layer, gg), rsum[:, g % 2, :, :], mv[:, g % 2, :, :], gg)
                g = group_at(s, i, "Q sum")
                if g is not None:
                    layer = g // NG
                    dve.wait_ge(g_ready, index["Q", g] + 1)
                    if g > 0:
                        dve.wait_ge(r1["Q"], g)
                    bank = ring("Q", g)
                    bias = vec[:, VBQ + layer:VBQ + layer + 1]
                    if g == 0:
                        dve.wait_ge(ld_vec, 16)
                    if layer == 0:
                        dve.wait_ge(*evacuated("A", g))
                        i_ = v.scalar_tensor_tensor(full["Q"][:, :], bank, bias, qscale[:, :], ALU.add, ALU.mult)
                    elif layer == 1:
                        if g == NG:
                            dve.wait_ge(mask_step, NG + 2)
                        i_ = v.scalar_tensor_tensor(
                            full["Q"][:, :].rearrange("p (b t) -> p b t", b=GB), bank.rearrange("p (b t) -> p b t", b=GB), bias,
                            cscale[:, GB * (g % NG):GB * (g % NG) + GB].unsqueeze(2).to_broadcast([128, GB, S]), ALU.add, ALU.mult)
                    else:
                        i_ = v.tensor_scalar(full["Q"][:, :], bank, bias, SCALE, ALU.add, ALU.mult)
                    i_.then_inc(dve_evac, 1)
                g = group_at(s, i, "F2 sum")
                if g is not None:
                    gg = g % NG
                    dve.wait_ge(g_ready, index["F2b", g] + 1)
                    dve.wait_ge(res_done, res_order.index(("F", gg)) + 1)
                    v.tensor_tensor(rsum[:, 2, :, :].rearrange("p b d -> p (b d)"), ring("F2a", gg + 2 * NG),
                                    res[:, GB * gg:GB * gg + GB, :].rearrange("p b d -> p (b d)"), ALU.add).then_inc(dve_evac, 1)
                g = group_at(s, i, "F stats")
                if g is not None:
                    dve.wait_ge(*evacuated("F2a", g))
                    for b in range(GB):
                        last = v.bn_stats(fstat[:, b, :], rsum[:, 2, b, :])
                    last.then_inc(fstat_done, 1)
                    dve.wait_ge(fstat_done, g - 2 * NG + 1)
                    for b in range(GB):
                        last = v.bn_aggr(fmv[:, b, :], fstat[:, b, :])
                    last.then_inc(fmv_done, 1)
                g = group_at(s, i, "F normalize")
                if g is not None:
                    dve.wait_ge(gain_done, norm_index(1, g % NG) + 2)
                    dve.wait_ge(fmv_done, g - 2 * NG + 1)
                    normalize(norm_index("F", g % NG), rsum[:, 2, :, :], fmv, g % NG)
                for m, stage, do in (("K", "K first", first_part), ("Q", "Q first", first_part), ("Q", "Q second", second_part)):
                    if group_at(s, i, stage) is not None:
                        do(m, group_at(s, i, stage))
                for g in range(1, NG):
                    if once(s, i, f"mask {g}"):
                        query_mask(g)
                if once(s, i, "key mask"):
                    key_mask()

        @block.gpsimd
        def _(pool):
            gp = nc.gpsimd
            def constants(n):
                gp.memset(vst[n][:, :, :].rearrange("p n e -> p (n e)"), 0.0).then_inc(blank, 1)
                pool.wait_ge(blank, n + 1)
                ones = vst[n][:, :, :].rearrange("p n (o e) -> p (n o) e", e=V_ODD)[:, :, 0:4 * 32]
                gp.memset(ones.rearrange("p n (c e) -> p n c e", e=32)[:, :, :, DK:DK + 1], 1.0).then_inc(const_ready, 1)
                gp.memset(qst[n][:, :, :].rearrange("p n t -> p (n t)").bitcast(F32), TWO_ONES).then_inc(q_ones[n], 1)

            def zeros(n):
                gp.memset(kst[n][:, :, :, :].rearrange("p n a t -> p (n a t)").bitcast(U32), 0).then_inc(zeroed[n], 1)

            constants(0)
            gp.memset(mhalf[:, :], -0.5)
            gp.memset(zrow[:, :], 0.0)

            def gain_row(j):
                return row[:, R_G + j, :].unsqueeze(1).to_broadcast([128, GB, D])

            def offset_row(j):
                return row[:, R_B + j, :].unsqueeze(1).to_broadcast([128, GB, D])

            def offsets():
                pool.wait_ge(ld_row, 16)
                for j in range(3):
                    last = gp.tensor_tensor(row[:, R_B + j, :], row[:, R_B + j, :], row[:, R_BO + j, :], ALU.add)
                last.then_inc(gain_done, 1)

            def residual_rows(g):
                pool.wait_ge(ld_res[g], 16)
                own = res[:, GB * g:GB * g + GB, :]
                gp.tensor_tensor(own, own, row[:, R_BOSA, :].unsqueeze(1).to_broadcast([128, GB, D]), ALU.add).then_inc(res_done, 1)

            def deviation(n, stats):
                if n > 1:
                    pool.wait_ge(norm_done, n - 1)
                gp.tensor_scalar(vareps[:, n % 2, :].unsqueeze(2), stats[:, :, 1:2], EPS, None, ALU.add).then_inc(vareps_done, 1)
                pool.wait_ge(vareps_done, n + 1)
                gp.tensor_tensor(rstd[:, n % 2, :], vareps[:, n % 2, :], mhalf[:, :], ALU.pow).then_inc(rstd_done, 1)

            def affine(n, layer, gg, half):
                j = {0: 0, 1: 1, "F": 2, 2: 3}[layer]
                if half == 0:
                    pool.wait_ge(norm_done, n + 1)
                if layer == 2:
                    dst = fin[:, gg % 2, :, :]
                    if gg >= 2 and half == 0:
                        pool.wait_ge(stored[gg % 2], 16 * (gg // 2))
                else:
                    dst = res[:, GB * gg:GB * gg + GB, :]
                if half == 0:
                    gp.tensor_tensor(dst, norm[:, GB * gg:GB * gg + GB, :], gain_row(j), ALU.mult).then_inc(gain_done, 1)
                    return
                pool.wait_ge(gain_done, n + 2)
                gp.tensor_tensor(dst, dst, offset_row(j), ALU.add).then_inc(fin_ready if layer == 2 else res_done, 1)

            for s, i in steps:
                u = unit_at(s, i, "max parts")
                if u is not None:
                    heads = negm[:, u % MAXIMA, :].rearrange("p (n a) -> p a n", a=2)
                    left = nrest[:, u % 2, :].rearrange("p (a n) -> p a n", a=2)
                    pt = [nparts[:, u % 2, n, :].rearrange("p (a n) -> p a n", a=2) for n in range(3)]
                    pool.wait_ge(max_done, CH * (u + 1))
                    if u > 1:
                        pool.wait_ge(mt_ready, u - 1)
                    gp.tensor_copy(pt[0], heads).then_inc(nparts_step, 1)
                    pool.wait_ge(nparts_step, 3 * u + 1)
                    gp.tensor_tensor(left, heads, pt[0], ALU.subtract).then_inc(nparts_step, 1)
                    pool.wait_ge(nparts_step, 3 * u + 2)
                    gp.tensor_copy(pt[1], left).then_inc(nparts_step, 1)
                    pool.wait_ge(nparts_step, 3 * u + 3)
                    gp.tensor_tensor(pt[2], left, pt[1], ALU.subtract).then_inc(nparts_done, 1)
                g = norm_at(s, i, "deviation")
                if g is not None:
                    pool.wait_ge(mv_done, 4 * g + 4)
                    deviation(norm_index(g // NG, g % NG), mv[:, g % 2, :, :])
                g = group_at(s, i, "F deviation")
                if g is not None:
                    pool.wait_ge(fmv_done, g - 2 * NG + 1)
                    deviation(norm_index("F", g % NG), fmv)
                for half in range(2):
                    g = norm_at(s, i, ("gain", "offset")[half])
                    if g is not None and g < GROUPS - 1:
                        affine(norm_index(g // NG, g % NG), g // NG, g % NG, half)
                    g = group_at(s, i, ("F gain", "F offset")[half])
                    if g is not None:
                        affine(norm_index("F", g % NG), "F", g % NG, half)
                if once(s, i, "offsets"):
                    offsets()
                for n in range(NG):
                    if once(s, i, f"residual rows {n}"):
                        residual_rows(n)
                for n in range(1, STACKS):
                    if once(s, i, f"constants {n}"):
                        constants(n)
                    if once(s, i, f"zeros {n}"):
                        zeros(n)
                for m in "KQ":
                    g = group_at(s, i, m + " rest")
                    if g is not None:
                        pool.wait_ge(p1[m], g + 1)
                        if g > 0:
                            pool.wait_ge(p2[m], g)
                            pool.wait_ge(p3[m], g)
                        gp.tensor_tensor(rest[m][:, :], full[m][:, :], part[m][:, 0, :], ALU.subtract).then_inc(r1[m], 1)
                for m in "KQ":
                    g = group_at(s, i, m + " third")
                    if g is not None:
                        pool.wait_ge(p2[m], g + 1)
                        gp.tensor_tensor(part[m][:, 2, :], rest[m][:, :], part[m][:, 1, :], ALU.subtract).then_inc(p3[m], 1)


def kernel(**inputs):
    import ml_dtypes as _ml
    import numpy as _np
    import concourse.bacc as _bacc
    from concourse import mybir as _mybir
    from concourse.bass_utils import run_bass_kernel_spmd as _run

    a = {k: _np.asarray(v) for k, v in inputs.items()}

    def to_rows(wt):
        return wt.reshape(PAIRS, 2, DK, D).transpose(3, 1, 2, 0).reshape(D, D)

    def to_col(bias):
        return bias.reshape(PAIRS, 2, DK).transpose(1, 2, 0).reshape(D, 1)

    att = [("L0_xattn_sa_w", "L0_xattn_sa_b"), ("L0_xattn_ca_w", "L0_xattn_ca_b"), ("L1_xattn_W", "L1_xattn_b")]
    def by_pair(m):
        return m.reshape(CH // 2, 2, 4, DK, -1).transpose(0, 2, 1, 3, 4).reshape(D, -1)

    weights = _np.concatenate(
        [m for wn, _ in att for m in (to_rows(a[wn + "q"]), to_rows(a[wn + "k"]), a[wn + "v"].T, by_pair(a[wn + "o"].T))]
        + [a["L0_xattn_ffn_w1"].T]
        + [a["L0_xattn_ffn_w2"].T.reshape(4, 128, D).transpose(1, 0, 2).reshape(128, FF)], axis=1)
    vectors = _np.concatenate(
        [to_col(a[bn + "q"]) for _, bn in att] + [to_col(a[bn + "k"]) for _, bn in att]
        + [by_pair(a[bn + "v"]) for _, bn in att]
        + [a["L0_xattn_ffn_b1"].reshape(4, 128).T]
        + [a[f"L0_xattn_ln{n}_g"].reshape(D, 1) for n in (1, 2, 3)]
        + [a[f"L0_xattn_ln{n}_b"].reshape(D, 1) for n in (1, 2, 3)], axis=1)
    rows = _np.stack(
        [a["L0_xattn_sa_bo"]] + [a[f"L0_xattn_ln{n}_g"] for n in (1, 2, 3)] + [a["L1_xattn_ln_gamma"]]
        + [a[f"L0_xattn_ln{n}_b"] for n in (1, 2, 3)] + [a["L1_xattn_ln_beta"]]
        + [a["L0_xattn_ca_bo"], a["L0_xattn_ffn_b2"], a["L1_xattn_bo"]])
    k_rows = _np.zeros((6, PAIRS, 2, GT), _ml.bfloat16)
    for n in range(3):
        for h in range(2):
            k_rows[2 * n + h, :, h, :] = 1
    arrays = {
        "x_tok": a["x"], "x_t": a["x"].transpose(2, 0, 1).reshape(D, B * S),
        "ctx_t": a["ctx_1024"].transpose(2, 0, 1).reshape(D, B * S),
        "mask_k": a["mask_Bx1x1xS2_if1"].reshape(B, S), "mask_qk": a["mask_Bx1xSxS2_if1"].reshape(B, S, S),
        "weights": weights, "vectors": vectors, "rows": rows, "k_rows": k_rows,
        "ident": _np.eye(128, dtype=_np.float32),
    }
    arrays = {k: _np.ascontiguousarray(v) for k, v in arrays.items()}
    nc = _bacc.Bacc("TRN2", target_bir_lowering=False, num_devices=1)
    args = [nc.dram_tensor("in_" + k, v.shape, _mybir.dt.from_np(v.dtype), kind="ExternalInput").ap() for k, v in arrays.items()]
    args.append(nc.dram_tensor("out_0", (B, S, D), _mybir.dt.float32, kind="ExternalOutput").ap())
    build(nc, *args)
    r = _run(nc, [{"in_" + k: v for k, v in arrays.items()}], core_ids=[0])
    return r.results[0]["out_0"]
```
